# Optimizing a Trainium2 kernel written in Bass

```python
import numpy as np
import jax
import jax.numpy as jnp

def _softmax(x, axis=-1):
    return jax.nn.softmax(x, axis=axis)

def _gelu(x):
    return jax.nn.gelu(x, approximate=True)

def _silu(x):
    return jax.nn.silu(x)

def _sigmoid(x):
    return jax.nn.sigmoid(x)

def _layernorm(x, axis=-1, eps=1e-05):
    m = jnp.mean(x, axis=axis, keepdims=True)
    v = jnp.var(x, axis=axis, keepdims=True)
    return (x - m) / jnp.sqrt(v + eps)

def _scatter_add(tgt, idx, src, axis=0):
    return tgt.at[idx].add(src)

def _segment_sum(src, seg, n):
    return jax.ops.segment_sum(src, seg, n)
kernel_name = 'mk_prb_d2_jaxref_r8_6015a4'

def setup_inputs(seed: int=0):
    np.random.seed(seed)
    _w = jnp.asarray

    def _L0_attn_setup():
        import jax, jax.numpy as jnp
        import numpy as np
        import math
        D_MODEL = 128
        LAYER_ID = 6
        NUM_LAYERS = 12
        B, T = (8, 256)
        MIN_P = -1e+38

        def _init_params():
            C = D_MODEL
            r01 = LAYER_ID / (NUM_LAYERS - 1)
            r1a0 = 1.0 - LAYER_ID / NUM_LAYERS
            h = np.arange(C, dtype=np.float32)
            decay_speed = -5.0 + 8.0 * (h / (C - 1)) ** (0.7 + 1.3 * r01)
            zigzag = ((np.arange(C) + 1) % 3 - 1).astype(np.float32) * 0.5
            U = np.float32(math.log(0.3)) + zigzag
            xx = (np.arange(C, dtype=np.float32) / C).reshape(1, 1, C)
            tmk = xx ** r1a0
            tmv = xx ** r1a0 + 0.3 * r01
            tmr = xx ** (0.5 * r1a0)
            return (jnp.asarray(decay_speed), jnp.asarray(U), jnp.asarray(tmk, jnp.float32), jnp.asarray(tmv, jnp.float32), jnp.asarray(tmr, jnp.float32))

        def _wkv(W, U, k, v):
            w = -jnp.exp(W)
            Bb, Tt, Cc = k.shape
            aa0 = jnp.zeros((Bb, Cc), k.dtype)
            bb0 = jnp.zeros((Bb, Cc), k.dtype)
            pp0 = jnp.full((Bb, Cc), MIN_P, k.dtype)

            def step(carry, kv_t):
                aa, bb, pp = carry
                kt, vt = kv_t
                ww = U + kt
                p = jnp.maximum(pp, ww)
                e1 = jnp.exp(pp - p)
                e2 = jnp.exp(ww - p)
                y = (e1 * aa + e2 * vt) / (e1 * bb + e2)
                ww2 = pp + w
                p2 = jnp.maximum(ww2, kt)
                e1b = jnp.exp(ww2 - p2)
                e2b = jnp.exp(kt - p2)
                return ((e1b * aa + e2b * vt, e1b * bb + e2b, p2), y)
            kT = jnp.swapaxes(k, 0, 1)
            vT = jnp.swapaxes(v, 0, 1)
            _, yT = jax.lax.scan(step, (aa0, bb0, pp0), (kT, vT))
            return jnp.swapaxes(yT, 0, 1)

        def _reference_tuple_inner(x, W, U, time_mix_k, time_mix_v, time_mix_r, Wk, Wv, Wr, Wo):
            xs = jnp.pad(x, ((0, 0), (1, 0), (0, 0)))[:, :-1]
            xk = x * time_mix_k + xs * (1.0 - time_mix_k)
            xv = x * time_mix_v + xs * (1.0 - time_mix_v)
            xr = x * time_mix_r + xs * (1.0 - time_mix_r)
            K = jnp.einsum('btc,dc->btd', xk, Wk)
            V = jnp.einsum('btc,dc->btd', xv, Wv)
            R = jnp.einsum('btc,dc->btd', xr, Wr)
            wkv = _wkv(W, U, K, V)
            hidden = jax.lax.stop_gradient(wkv[:, -1, :])
            rwkv = jax.nn.sigmoid(R) * wkv
            output = jnp.einsum('btc,dc->btd', rwkv, Wo)
            return (output, hidden)
        key = jax.random.key(seed)
        k0, k1, k2, k3, k4 = jax.random.split(key, 5)
        W, U, tmk, tmv, tmr = _init_params()
        C = D_MODEL
        s = 1.0 / math.sqrt(C)
        return {'x': jax.random.normal(k0, (B, T, C), jnp.float32), 'W': W, 'U': U, 'time_mix_k': tmk, 'time_mix_v': tmv, 'time_mix_r': tmr, 'Wk': jax.random.normal(k1, (C, C), jnp.float32) * s, 'Wv': jax.random.normal(k2, (C, C), jnp.float32) * s, 'Wr': jax.random.normal(k3, (C, C), jnp.float32) * s, 'Wo': jax.random.normal(k4, (C, C), jnp.float32) * s}
    _L0_attn_in = _L0_attn_setup()

    def _L0_ffn_setup():
        import jax, jax.numpy as jnp
        import numpy as np
        B, S, H, F, E = (4, 256, 128, 512, 8)
        key = jax.random.key(seed)
        ks = jax.random.split(key, 8)
        s = 1.0 / np.sqrt(H)
        sf = 1.0 / np.sqrt(F)
        return {'x': jax.random.normal(ks[0], (B, S, H), jnp.float32), 'wr': jax.random.uniform(ks[1], (H, E), jnp.float32, -s, s), 'br': jax.random.uniform(ks[2], (E,), jnp.float32, -s, s), 'w1': jax.random.uniform(ks[3], (E, H, F), jnp.float32, -s, s), 'b1': jax.random.uniform(ks[4], (E, F), jnp.float32, -s, s), 'w2': jax.random.uniform(ks[5], (E, F, H), jnp.float32, -sf, sf), 'b2': jax.random.uniform(ks[6], (E, H), jnp.float32, -sf, sf)}
    _L0_ffn_in = _L0_ffn_setup()

    def _L1_attn_setup():
        import jax, jax.numpy as jnp
        import numpy as np
        EMBED_DIM = 128
        N_HEADS = 16
        HEAD_DIM = EMBED_DIM // N_HEADS
        B, T = (1, 512)
        key = jax.random.key(seed)
        k1, k2, k3 = jax.random.split(key, 3)
        x = jax.random.normal(k1, (B, T, EMBED_DIM), dtype=jnp.float32)
        w_qkv = jax.random.normal(k2, (EMBED_DIM, 3 * EMBED_DIM), dtype=jnp.float32) * EMBED_DIM ** (-0.5)
        w_out = jax.random.normal(k3, (EMBED_DIM, EMBED_DIM), dtype=jnp.float32) * EMBED_DIM ** (-0.5)
        return {'x': x, 'w_qkv': w_qkv, 'w_out': w_out}
    _L1_attn_in = _L1_attn_setup()

    def _L1_ffn_setup():
        import jax, jax.numpy as jnp
        import numpy as np
        DIM = 128

        def _reference_tuple_inner(x, W_r, W_k, W_v, mu_r, mu_k):
            B, T, C = x.shape
            x_prev = jnp.concatenate([jnp.zeros((B, 1, C), x.dtype), x[:, :-1, :]], axis=1)
            xr = mu_r * x + (1.0 - mu_r) * x_prev
            xk = mu_k * x + (1.0 - mu_k) * x_prev
            r = jax.nn.sigmoid(jnp.einsum('btc,dc->btd', xr, W_r))
            k = jnp.einsum('btc,dc->btd', xk, W_k)
            k_act = jnp.square(jax.nn.relu(k))
            out = r * jnp.einsum('btc,dc->btd', k_act, W_v)
            new_state = x[:, -1, :]
            return (out, new_state)
        key = jax.random.key(seed)
        ks = jax.random.split(key, 6)
        B, T, C = (8, 256, DIM)
        x = jax.random.normal(ks[0], (B, T, C), dtype=jnp.float32)
        s = 1.0 / np.sqrt(C)
        W_r = jax.random.uniform(ks[1], (C, C), jnp.float32, -s, s)
        W_k = jax.random.uniform(ks[2], (C, C), jnp.float32, -s, s)
        W_v = jax.random.uniform(ks[3], (C, C), jnp.float32, -s, s)
        mu_r = jax.random.uniform(ks[4], (C,), jnp.float32)
        mu_k = jax.random.uniform(ks[5], (C,), jnp.float32)
        return {'x': x, 'W_r': W_r, 'W_k': W_k, 'W_v': W_v, 'mu_r': mu_r, 'mu_k': mu_k}
    _L1_ffn_in = _L1_ffn_setup()
    _d = {'L0_attn_x': _L0_attn_in['x'], 'L0_attn_W': _L0_attn_in['W'], 'L0_attn_U': _L0_attn_in['U'], 'L0_attn_time_mix_k': _L0_attn_in['time_mix_k'], 'L0_attn_time_mix_v': _L0_attn_in['time_mix_v'], 'L0_attn_time_mix_r': _L0_attn_in['time_mix_r'], 'L0_attn_Wk': _L0_attn_in['Wk'], 'L0_attn_Wv': _L0_attn_in['Wv'], 'L0_attn_Wr': _L0_attn_in['Wr'], 'L0_attn_Wo': _L0_attn_in['Wo'], 'L0_ffn_wr': _L0_ffn_in['wr'], 'L0_ffn_br': _L0_ffn_in['br'], 'L0_ffn_w1': _L0_ffn_in['w1'], 'L0_ffn_b1': _L0_ffn_in['b1'], 'L0_ffn_w2': _L0_ffn_in['w2'], 'L0_ffn_b2': _L0_ffn_in['b2'], 'L1_attn_w_qkv': _L1_attn_in['w_qkv'], 'L1_attn_w_out': _L1_attn_in['w_out'], 'L1_ffn_W_r': _L1_ffn_in['W_r'], 'L1_ffn_W_k': _L1_ffn_in['W_k'], 'L1_ffn_W_v': _L1_ffn_in['W_v'], 'L1_ffn_mu_r': _L1_ffn_in['mu_r'], 'L1_ffn_mu_k': _L1_ffn_in['mu_k']}
    _x0 = _d['L0_attn_x']
    _d['L0_attn_x'] = jax.random.normal(jax.random.fold_in(jax.random.key(seed), 1), (1, 2048, 128), dtype=_x0.dtype)
    del _x0
    return _d

def reference(L0_attn_x, L0_attn_W, L0_attn_U, L0_attn_time_mix_k, L0_attn_time_mix_v, L0_attn_time_mix_r, L0_attn_Wk, L0_attn_Wv, L0_attn_Wr, L0_attn_Wo, L0_ffn_wr, L0_ffn_br, L0_ffn_w1, L0_ffn_b1, L0_ffn_w2, L0_ffn_b2, L1_attn_w_qkv, L1_attn_w_out, L1_ffn_W_r, L1_ffn_W_k, L1_ffn_W_v, L1_ffn_mu_r, L1_ffn_mu_k):

    def _L0_attn_ref(x, W, U, time_mix_k, time_mix_v, time_mix_r, Wk, Wv, Wr, Wo):
        import jax, jax.numpy as jnp
        import numpy as np
        import math
        D_MODEL = 128
        LAYER_ID = 6
        NUM_LAYERS = 12
        B, T = (8, 256)
        MIN_P = -1e+38

        def _init_params():
            C = D_MODEL
            r01 = LAYER_ID / (NUM_LAYERS - 1)
            r1a0 = 1.0 - LAYER_ID / NUM_LAYERS
            h = np.arange(C, dtype=np.float32)
            decay_speed = -5.0 + 8.0 * (h / (C - 1)) ** (0.7 + 1.3 * r01)
            zigzag = ((np.arange(C) + 1) % 3 - 1).astype(np.float32) * 0.5
            U = np.float32(math.log(0.3)) + zigzag
            xx = (np.arange(C, dtype=np.float32) / C).reshape(1, 1, C)
            tmk = xx ** r1a0
            tmv = xx ** r1a0 + 0.3 * r01
            tmr = xx ** (0.5 * r1a0)
            return (jnp.asarray(decay_speed), jnp.asarray(U), jnp.asarray(tmk, jnp.float32), jnp.asarray(tmv, jnp.float32), jnp.asarray(tmr, jnp.float32))

        def _wkv(W, U, k, v):
            w = -jnp.exp(W)
            Bb, Tt, Cc = k.shape
            aa0 = jnp.zeros((Bb, Cc), k.dtype)
            bb0 = jnp.zeros((Bb, Cc), k.dtype)
            pp0 = jnp.full((Bb, Cc), MIN_P, k.dtype)

            def step(carry, kv_t):
                aa, bb, pp = carry
                kt, vt = kv_t
                ww = U + kt
                p = jnp.maximum(pp, ww)
                e1 = jnp.exp(pp - p)
                e2 = jnp.exp(ww - p)
                y = (e1 * aa + e2 * vt) / (e1 * bb + e2)
                ww2 = pp + w
                p2 = jnp.maximum(ww2, kt)
                e1b = jnp.exp(ww2 - p2)
                e2b = jnp.exp(kt - p2)
                return ((e1b * aa + e2b * vt, e1b * bb + e2b, p2), y)
            kT = jnp.swapaxes(k, 0, 1)
            vT = jnp.swapaxes(v, 0, 1)
            _, yT = jax.lax.scan(step, (aa0, bb0, pp0), (kT, vT))
            return jnp.swapaxes(yT, 0, 1)

        def _reference_tuple_inner(x, W, U, time_mix_k, time_mix_v, time_mix_r, Wk, Wv, Wr, Wo):
            xs = jnp.pad(x, ((0, 0), (1, 0), (0, 0)))[:, :-1]
            xk = x * time_mix_k + xs * (1.0 - time_mix_k)
            xv = x * time_mix_v + xs * (1.0 - time_mix_v)
            xr = x * time_mix_r + xs * (1.0 - time_mix_r)
            K = jnp.einsum('btc,dc->btd', xk, Wk)
            V = jnp.einsum('btc,dc->btd', xv, Wv)
            R = jnp.einsum('btc,dc->btd', xr, Wr)
            wkv = _wkv(W, U, K, V)
            hidden = jax.lax.stop_gradient(wkv[:, -1, :])
            rwkv = jax.nn.sigmoid(R) * wkv
            output = jnp.einsum('btc,dc->btd', rwkv, Wo)
            return (output, hidden)
        return _reference_tuple_inner(x, W, U, time_mix_k, time_mix_v, time_mix_r, Wk, Wv, Wr, Wo)[0]

    def _L0_ffn_ref(x, wr, br, w1, b1, w2, b2):
        import jax, jax.numpy as jnp
        import numpy as np
        B, S, H, F, E = (4, 256, 128, 512, 8)
        scores = jnp.einsum('bsh,he->bse', x, wr) + br
        expert_id = jnp.argmax(scores, axis=-1)
        h = jnp.einsum('bsh,ehf->ebsf', x, w1) + b1[:, None, None, :]
        h = jax.nn.gelu(h, approximate=False)
        y = jnp.einsum('ebsf,efh->ebsh', h, w2) + b2[:, None, None, :]
        one_hot = jax.nn.one_hot(expert_id, E, dtype=x.dtype)
        out = jnp.einsum('ebsh,bse->bsh', y, one_hot)
        return out

    def _L1_attn_ref(x, w_qkv, w_out):
        import jax, jax.numpy as jnp
        import numpy as np
        EMBED_DIM = 128
        N_HEADS = 16
        HEAD_DIM = EMBED_DIM // N_HEADS
        B, T = (1, 512)
        b, t, c = x.shape
        qkv = x @ w_qkv
        q, k, v = jnp.split(qkv, 3, axis=-1)

        def heads(a):
            return a.reshape(b, t, N_HEADS, HEAD_DIM).transpose(0, 2, 1, 3)
        q, k, v = (heads(q), heads(k), heads(v))
        scale = 1.0 / jnp.sqrt(jnp.asarray(HEAD_DIM, dtype=x.dtype))
        att = jnp.einsum('bhqd,bhkd->bhqk', q, k) * scale
        att = jax.nn.softmax(att, axis=-1)
        y = jnp.einsum('bhqk,bhkd->bhqd', att, v)
        y = y.transpose(0, 2, 1, 3).reshape(b, t, c)
        return y @ w_out

    def _L1_ffn_ref(x, W_r, W_k, W_v, mu_r, mu_k):
        import jax, jax.numpy as jnp
        import numpy as np
        DIM = 128

        def _reference_tuple_inner(x, W_r, W_k, W_v, mu_r, mu_k):
            B, T, C = x.shape
            x_prev = jnp.concatenate([jnp.zeros((B, 1, C), x.dtype), x[:, :-1, :]], axis=1)
            xr = mu_r * x + (1.0 - mu_r) * x_prev
            xk = mu_k * x + (1.0 - mu_k) * x_prev
            r = jax.nn.sigmoid(jnp.einsum('btc,dc->btd', xr, W_r))
            k = jnp.einsum('btc,dc->btd', xk, W_k)
            k_act = jnp.square(jax.nn.relu(k))
            out = r * jnp.einsum('btc,dc->btd', k_act, W_v)
            new_state = x[:, -1, :]
            return (out, new_state)
        return _reference_tuple_inner(x, W_r, W_k, W_v, mu_r, mu_k)[0]
    x = L0_attn_x
    xn = _layernorm(x, axis=-1)
    x = x + _L0_attn_ref(xn, L0_attn_W, L0_attn_U, L0_attn_time_mix_k, L0_attn_time_mix_v, L0_attn_time_mix_r, L0_attn_Wk, L0_attn_Wv, L0_attn_Wr, L0_attn_Wo) + _L0_ffn_ref(xn, L0_ffn_wr, L0_ffn_br, L0_ffn_w1, L0_ffn_b1, L0_ffn_w2, L0_ffn_b2)
    xn = _layernorm(x, axis=-1)
    x = x + _L1_attn_ref(xn, L1_attn_w_qkv, L1_attn_w_out) + _L1_ffn_ref(xn, L1_ffn_W_r, L1_ffn_W_k, L1_ffn_W_v, L1_ffn_mu_r, L1_ffn_mu_k)
    return x

_drawn_inputs = setup_inputs


def setup_inputs(seed=0):
    import zlib

    import numpy as np

    out = dict(_drawn_inputs(seed))
    spreads = {}
    factors = {'L0_ffn_b1': 3.115, 'L1_ffn_W_r': 3.238, 'L1_ffn_mu_r': 6.558}
    for name, (base, spread) in spreads.items():
        noise = np.random.default_rng([zlib.crc32(name.encode()), seed]).standard_normal(out[name].shape)
        drawn = base * np.exp(spread * noise) if base else spread * noise
        out[name] = jnp.asarray(drawn.astype(out[name].dtype))
    for name, factor in factors.items():
        out[name] = (out[name] * factor).astype(out[name].dtype)
    return out
```

```python
import concourse.bass as bass
from concourse import mybir
from contextlib import ExitStack


def two_layer_kernel(nc: bass.Bass, x, vecs, w_t, router_w, router_b, expert_w, expert_b2, w_qkv, w_out, out):
    fp32, bf16 = mybir.dt.float32, mybir.dt.bfloat16
    i32, u32 = mybir.dt.int32, mybir.dt.uint32
    ALU, ACT, AX = mybir.AluOpType, mybir.ActivationFunctionType, mybir.AxisListType

    P = 128
    T, C = x.shape[1], x.shape[2]
    NT = T // P
    CH = 512
    NC = T // CH
    TPC = CH // P
    E = router_w.shape[1]
    F = (expert_w.shape[2] - C) // 1
    F = 512
    NF = F // P
    EW = expert_w.shape[2]
    RING = 3
    MT = NT + E
    assert MT % RING == 0
    ROWS = MT * P
    XW = C + 4
    H, HD = 16, 8
    G, HG = 4, 4
    NKT = T // P
    NQ = T // CH
    SCALE = float(HD) ** -0.5
    NEG = -1e38
    EPS = 1e-5
    SAFE = 226.0

    x_t = x.rearrange("a (n p) c -> p (a n) c", p=P)
    out_t = out.rearrange("a (n p) c -> p (a n) c", p=P)
    routed = nc.dram_tensor("routed", (ROWS, XW), fp32, kind="Internal").ap()
    moe = nc.dram_tensor("moe", (T, C), fp32, kind="Internal").ap()
    moe_t = moe.rearrange("(n p) c -> p n c", p=P)
    NB = 6
    stacked = nc.dram_tensor("stacked", (2, C, NB, T), bf16, kind="Internal").ap()
    shifts = nc.dram_tensor("shifts", (H, 2, T), bf16, kind="Internal").ap()
    ROW0 = 8

    ctx = ExitStack()
    with ctx:
        def sb(name, shape, dt=fp32):
            return ctx.enter_context(nc.sbuf_tensor(name, shape, dt))

        def sem(name):
            return ctx.enter_context(nc.semaphore(name))

        psum = ctx.enter_context(nc.psum_tensor("psum", [P, 8, CH], fp32))
        bank = [psum[:, i, :] for i in range(8)]

        xs = sb("xs", [P, NT, C])
        xn = sb("xn", [P, NT, XW])
        xnT = sb("xnT", [P, T + 1])
        buf_a = sb("buf_a", [P, T])
        buf_b = sb("buf_b", [P, NT * C])
        ident = sb("ident", [P, P])
        ones = sb("ones", [P, P])
        before = sb("before", [P, P])
        vec = sb("vec", [P, 7])
        wts = sb("wts", [P, 7, C])
        mix = sb("mix", [P, 5, 2, C])
        wqkv = sb("wqkv", [P, 3 * C])
        wo1 = sb("wo1", [P, C])
        stats = sb("stats", [P, NT, 6])
        mv = sb("mv", [P, NT, 2])
        veps = sb("veps", [P, NT])
        halves = sb("halves", [P, NT])
        rstd = sb("rstd", [P, NT])
        zero = sb("zero", [P, XW])

        k_stack = sb("k_stack", [P, H, T], bf16)
        q_stack = sb("q_stack", [P, H // 2, T], bf16)
        probs = sb("probs", [P, 4, HG, CH])
        v_aug = sb("v_aug", [P, NKT, H, HD + 1])
        yT = xn[:, :, :].rearrange("p n c -> p (n c)")[:, 0:T]
        y_g = sb("y_g", [P, 2, CH])
        y_den = sb("y_den", [P, CH])

        ks32 = k_stack[:, :, :].rearrange("p h t -> p (h t)").bitcast(fp32)
        arg = ks32[:, 0:4 * T].rearrange("p (j a t) -> p j a t", j=NC, a=4)
        kf, vf, ef, dd = (ks32[:, (4 + i) * T:(5 + i) * T] for i in range(4))
        pr32 = probs[:, :, :, :].rearrange("p a h t -> p (a h t)")
        m_run, a_run, b_run = (pr32[:, i * (T + 1):(i + 1) * (T + 1)] for i in range(3))
        tmp = pr32[:, 3 * (T + 1):3 * (T + 1) + CH]
        tmp2 = pr32[:, 3 * (T + 1) + CH:3 * (T + 1) + 2 * CH]
        qs32 = q_stack[:, :, :].rearrange("p h t -> p (h t)").bitcast(fp32)
        at = [0]

        def part(words):
            at[0] += words
            return qs32[:, at[0] - words:at[0]]

        ew = part(RING * EW).rearrange("p (s n) -> p s n", s=RING)
        xr = part(RING * XW).rearrange("p (s n) -> p s n", s=RING)
        xrT = part(RING * P).rearrange("p (s n) -> p s n", s=RING)
        hT = part(RING * F).rearrange("p (s n) -> p s n", s=RING)
        ye = part(RING * C).rearrange("p (s n) -> p s n", s=RING)
        eb2 = part(RING * C).rearrange("p (s n) -> p s n", s=RING)
        assert at[0] <= qs32.shape[1]

        rb = sb("rb", [P, E])
        rw = sb("rw", [P, E])
        score = sb("score", [P, NT, E])
        best = sb("best", [P, NT])
        rev = sb("rev", [P, E])
        hot = sb("hot", [P, NT, E])
        tot = sb("tot", [P, E, NT])
        cum = sb("cum", [P, E, NT])
        cnt = sb("cnt", [P, E])
        full = sb("full", [P, NT])
        over = sb("over", [P, E, NT])
        ntile = sb("ntile", [P, E])
        tend = sb("tend", [P, E])
        adj = sb("adj", [P, E])
        slotf = sb("slotf", [P, NT])
        slot = sb("slot", [P, NT], u32)
        tidx = sb("tidx", [1, MT])
        tge = sb("tge", [1, MT, E])
        tef = sb("tef", [1, MT])
        te = sb("te", [1, MT], i32)
        pad_id = sb("pad_id", [P, MT], i32)
        decay = sb("decay", [P, 1])

        at[0] = 0

        def ppart(words):
            at[0] += words
            return pr32[:, at[0] - words:at[0]]

        piece = ppart(4 * 3 * CH // 2).bitcast(bf16).rearrange("p (r s k t) -> p r s k t", r=2, s=2, k=3)
        left = ppart(CH)
        sq = ppart(2 * CH).rearrange("p (s t) -> p s t", s=2)
        norm = ppart(T)[0:H, :]
        assert at[0] <= pr32.shape[1]
        shiftp = xn[:, :, :].rearrange("p n c -> p (n c)")[0:H, 0:T].bitcast(bf16).rearrange("h (k t) -> h k t", k=2)
        top = sq.rearrange("p s t -> p (s t)")[:, 0:NT * H].rearrange("p (n h) -> p n h", n=NT)
        headsel = sb("headsel", [P, H])
        nmax = sb("nmax", [H, 2, NC])
        nbest = sb("nbest", [H, 3])
        flagf = sb("flagf", [1, 1])
        flag = sb("flag", [1, 1], i32)

        names = """vec_in wts_in wq_in const_in routed_zeroed pool_step dve_step ident_ready decay_exp mix_ready ln_var ln_rstd xn_ready
            xT_mm xT_ready router_mm hot_ready prefix_mm slots_ready k_mm v_mm r_mm k_ready v_ready e_ready
            wkv_args wkv_exps wkv_scans wkv_pool rwkv_ready scattered moe_xT_mm moe_xT_ready moe_h_mm moe_h_ready
            moe_y_mm moe_y_ready moe_turn shuffle_turn moe_in attn_mm x1_ready
            act_step q_mm k2_mm v2_mm q_split norm_mm norms_read flag_mm flag_ready v_aug_ready kv_zeroed q_zeroed
            piece_ready shift_ready shift_mid shift_in sq_ready gmax_mm gmax_read gmax_turned stack_set
            fk_mm fr_mm fkv_mm relu_ready kact_ready fe_ready fkv_ready z_ready
            scores_mm exps_done pv_mm acc_zeroed acc_free y_ready proj_mm""".split()
        S = {n: sem(n) for n in names}
        x_in = [sem(f"x_in{j}") for j in range(NC)]
        slot_in = [sem(f"slot_in{s}") for s in range(RING)]
        moe_out = [sem(f"moe_out{s}") for s in range(RING)]
        mid = [sem(f"mid{i}") for i in range(2)]
        stack_in = sem("stack_in")
        y_packed = [sem(f"y_packed{i}") for i in range(2)]
        done_out = sem("done_out")
        block = ctx.enter_context(nc.Block())

        @block.sync
        def _(sp):
            for j in range(NC):
                sp.dma_start(xs[:, TPC * j:TPC * (j + 1), :], x_t[:, TPC * j:TPC * (j + 1), :]).then_inc(x_in[j], 16)
            sp.dma_start(rw[:, :], router_w).then_inc(S["const_in"], 16)
            sp.dma_start(rb[:, :], router_b.partition_broadcast(P)).then_inc(S["const_in"], 16)
            sp.dma_start(vec[:, :], vecs).then_inc(S["vec_in"], 16)
            sp.dma_start(wts[:, :, :], w_t.rearrange("p (m n) -> p m n", m=7)).then_inc(S["wts_in"], 16)
            sp.dma_start(wqkv[:, :], w_qkv).then_inc(S["wq_in"], 16)
            sp.dma_start(wo1[:, :], w_out).then_inc(S["wq_in"], 16)
            sp.wait_ge(S["ident_ready"], 1)
            rt = routed.rearrange("(m p) c -> p m c", p=P)
            sp.dma_start(rt, zero[:, :].rearrange("p (a c) -> p a c", a=1).to_broadcast([P, MT, XW])).then_inc(S["routed_zeroed"], 16)
            sp.wait_ge(S["routed_zeroed"], 16)
            with nc.allow_non_contiguous_dma(reason="one word of each row"):
                sp.dma_start(rt[:, :, C:C + 1].bitcast(i32), pad_id[:, :].rearrange("p (m a) -> p m a", a=1)).then_inc(S["routed_zeroed"], 16)

            def load_tile(i, s):
                e = sp.value_load(te[0:1, bass.ds(i, 1)], min_val=0, max_val=E - 1)
                sp.dma_start(ew[:, s, :], expert_w[bass.ds(e, 1), :, :].rearrange("a p n -> p (a n)")).then_inc(slot_in[s], 16)
                sp.dma_start(eb2[0:1, s, :], expert_b2[bass.ds(e, 1), :]).then_inc(slot_in[s], 16)
                sp.dma_start(xr[:, s, :], routed[bass.ds(i * P, P), :]).then_inc(slot_in[s], 16)

            sp.wait_ge(S["slots_ready"], 1)
            sp.wait_ge(S["scattered"], 16 * NT)
            for i in range(RING):
                load_tile(i, i)
            with sp.Fori(0, MT // RING - 1) as r:
                for s in range(RING):
                    sp.wait_ge(S["moe_y_mm"], r * RING + s + 1)
                    sp.wait_ge(moe_out[s], r * 16 + 16)
                    sp.wait_ge(slot_in[s], r * 48 + 48)
                    load_tile(r * RING + RING + s, s)
            for s in range(RING):
                sp.wait_ge(moe_out[s], 16 * (MT // RING))
            sp.dma_start(buf_b[:, :].rearrange("p (n c) -> p n c", n=NT), moe_t).then_inc(S["moe_in"], 16)
            for j in range(NC):
                c = slice(CH * j, CH * (j + 1))
                for s in range(2):
                    sp.wait_ge(S["piece_ready"], 2 * j + s + 1)
                    p = piece[:, j % 2, s]
                    if s == 0:
                        for k, b, m in ((0, 0, 3), (1, 3, 2), (2, 5, 1)):
                            sp.dma_start(stacked[0, :, b:b + m, c], p[:, k:k + 1, :].to_broadcast([P, m, CH])).then_inc(mid[s], 16)
                    else:
                        for b, m in ((0, 3), (3, 2), (5, 1)):
                            sp.dma_start(stacked[1, :, b:b + m, c], p[:, 0:m, :]).then_inc(mid[s], 16)
                if j == 0:
                    sp.wait_ge(S["q_zeroed"], 1)
                    sp.wait_ge(S["kv_zeroed"], 1)
                for s in range(2):
                    sp.wait_ge(mid[s], 48 * (j + 1))
                    for half in range(2):
                        rows = slice(64 * half + ROW0, 64 * half + ROW0 + NB * HD)
                        src = stacked[s].rearrange("(g a d) b t -> a (d b) g t", a=2, d=HD)[half, :, :, c]
                        dst = q_stack[rows, :, c] if s == 0 else k_stack[rows, half:H:2, c]
                        sp.dma_start(dst, src).then_inc(stack_in, 16)
            sp.wait_ge(S["shift_ready"], 1)
            sp.dma_start(shifts, shiftp).then_inc(S["shift_mid"], 16)
            sp.wait_ge(S["shift_mid"], 16)
            for half in range(2):
                sp.dma_start(q_stack[64 * half:64 * half + 2, :, :],
                             shifts.rearrange("(g a) k t -> a k g t", a=2)[half]).then_inc(S["shift_in"], 16)
            with sp.Fori(0, NQ) as r:
                for g in range(G):
                    sp.wait_ge(S["y_ready"], r * G + g + 1)
                    for h in range(HG):
                        sp.dma_start(yT[32 * g + HD * h:32 * g + HD * (h + 1), bass.ds(r * CH, CH)],
                                     y_g[32 * h:32 * h + HD, g % 2, :]).then_inc(y_packed[g % 2], 16)
            for j in range(NC):
                sp.wait_ge(S["x1_ready"], NC + j + 1)
                sp.dma_start(out_t[:, TPC * j:TPC * (j + 1), :], xs[:, TPC * j:TPC * (j + 1), :]).then_inc(done_out, 16)
            sp.wait_ge(done_out, 16 * NC)

        @block.gpsimd
        def _(pool):
            n = [0]

            def step(ins):
                n[0] += 1
                ins.then_inc(S["pool_step"], 1)

            def settle():
                pool.wait_ge(S["pool_step"], n[0])

            step(pool.memset(zero[:, :], 0.0))
            step(pool.memset(ones[:, :], 1.0))
            step(pool.memset(halves[:, :], -0.5))
            step(pool.iota(pad_id[:, :], pattern=[[P, MT]], base=T, channel_multiplier=1))
            step(pool.iota(xn[:, :, C:C + 1].bitcast(i32), pattern=[[P, NT]], base=0, channel_multiplier=1))
            step(pool.iota(rev[:, :], pattern=[[-1, E]], base=E, channel_multiplier=0, allow_small_or_imprecise_dtypes=True))
            step(pool.iota(full[:, :], pattern=[[P, NT]], base=0, channel_multiplier=0, allow_small_or_imprecise_dtypes=True))
            step(pool.iota(tidx[:, :], pattern=[[1, MT]], base=0, channel_multiplier=0, allow_small_or_imprecise_dtypes=True))
            step(pool.memset(xn[:, :, C + 1:XW], 0.0))
            settle()
            step(pool.affine_select(out=ident[:, :], in_=ones[:, :], compare_op=ALU.is_equal, fill=0.0,
                                    base=0, pattern=[[-1, P]], channel_multiplier=1))
            step(pool.affine_select(out=before[:, :], in_=ones[:, :], compare_op=ALU.is_gt, fill=0.0,
                                    base=0, pattern=[[1, P]], channel_multiplier=-1))
            settle()
            pool.sem_inc(S["ident_ready"], 1)
            step(pool.affine_select(out=headsel[:, :], in_=ones[:, 0:H], compare_op=ALU.is_ge, fill=0.0,
                                    base=0, pattern=[[-HD, H]], channel_multiplier=1))
            settle()
            step(pool.affine_select(out=headsel[:, :], in_=headsel[:, :], compare_op=ALU.is_ge, fill=0.0,
                                    base=HD - 1, pattern=[[HD, H]], channel_multiplier=-1))
            step(pool.memset(v_aug[:, :, :, HD:HD + 1], 1.0))

            def rsqrt(j):
                pool.wait_ge(S["ln_var"], j + 1)
                g = slice(TPC * (j % NC), TPC * (j % NC) + TPC)
                pool.tensor_tensor(rstd[:, g], veps[:, g], halves[:, g], ALU.pow).then_inc(S["ln_rstd"], 1)

            def mix_weight(j, w, v):
                step(pool.tensor_scalar(mix[:, j, 0, :], wts[:, w, :], vec[:, v:v + 1], None, ALU.mult))
                settle()
                pool.tensor_tensor(mix[:, j, 1, :], wts[:, w, :], mix[:, j, 0, :], ALU.subtract).then_inc(S["mix_ready"], 1)

            for j in range(NC):
                rsqrt(j)
                if j == 0:
                    pool.wait_ge(S["vec_in"], 16)
                    pool.wait_ge(S["wts_in"], 16)
                if j < 3:
                    mix_weight(j, (0, 1, 2)[j], (2, 3, 4)[j])
            mix_weight(3, 4, 5)
            mix_weight(4, 5, 6)
            pool.wait_ge(S["slots_ready"], 1)
            pool.wait_ge(S["routed_zeroed"], 32)
            for t in range(NT):
                pool.indirect_dma_start(routed, bass.IndirectOffsetOnAxis(ap=slot[:, t:t + 1], axis=0),
                                        xn[:, t, :], None, bounds_check=ROWS - 1, oob_is_err=False).then_inc(S["scattered"], 16)
            for j in range(NC):
                pool.wait_ge(S["wkv_scans"], j + 1)
                c = slice(CH * j, CH * (j + 1))
                pool.tensor_tensor(arg[:, j, 1, :], arg[:, j, 3, :], vf[:, c], ALU.mult).then_inc(S["wkv_pool"], 1)
                pool.tensor_tensor(arg[:, j, 0, :], arg[:, j, 2, :], b_run[:, c], ALU.mult).then_inc(S["wkv_pool"], 1)

            with pool.Fori(0, MT // RING) as r:
                for s in range(RING):
                    i = r * RING + s
                    pool.wait_ge(slot_in[s], r * 48 + 48)
                    pool.wait_ge(S["moe_y_ready"], i + 1)
                    pool.sem_inc(S["moe_turn"], 1)
                    pool.indirect_dma_start(moe, bass.IndirectOffsetOnAxis(ap=xr[:, s, C:C + 1].bitcast(u32), axis=0),
                                            ye[:, s, :], None, bounds_check=T - 1, oob_is_err=False).then_inc(moe_out[s], 16)

            pool.wait_ge(S["attn_mm"], NC)
            k_words = k_stack[:, :, :].rearrange("p h t -> p (h t)").bitcast(fp32)
            step(pool.memset(k_words, 0.0))
            settle()
            step(pool.memset(k_stack[0:2, 0:H:2, :], 1.0))
            step(pool.memset(k_stack[64:66, 1:H:2, :], 1.0))
            settle()
            pool.sem_inc(S["kv_zeroed"], 1)
            for s in range(RING):
                pool.wait_ge(moe_out[s], 16 * (MT // RING))
            step(pool.memset(qs32, 0.0))
            settle()
            pool.sem_inc(S["q_zeroed"], 1)
            for j in range(NC, 2 * NC):
                rsqrt(j)
            for j in range(NC):
                pool.wait_ge(S["relu_ready"], j + 1)
                c = slice(CH * j, CH * (j + 1))
                pool.tensor_tensor(buf_a[:, c], buf_a[:, c], buf_a[:, c], ALU.mult).then_inc(S["kact_ready"], 1)

        @block.scalar
        def _(act):
            act.wait_ge(S["vec_in"], 16)
            act.activation(decay[:, :], vec[:, 0:1], ACT.Exp).then_inc(S["decay_exp"], 1)
            for j in range(NC):
                act.wait_ge(S["xT_mm"], j + 1)
                act.activation(xnT[:, 1 + CH * j:1 + CH * (j + 1)], bank[j % 2], ACT.Copy).then_inc(S["xT_ready"], 1)
            for j in range(NC):
                c = slice(CH * j, CH * (j + 1))
                act.wait_ge(S["k_mm"], j + 1)
                act.activation(kf[:, c], bank[2], ACT.Copy).then_inc(S["k_ready"], 1)
                act.wait_ge(S["v_mm"], j + 1)
                act.activation(vf[:, c], bank[3], ACT.Copy).then_inc(S["v_ready"], 1)
                act.wait_ge(S["r_mm"], j + 1)
                act.activation(ef[:, c], bank[4], ACT.Exp, scale=-1.0).then_inc(S["e_ready"], 1)
                if j >= 1:
                    act.wait_ge(S["wkv_args"], j)
                    act.activation(arg[:, j - 1, :, :], arg[:, j - 1, :, :], ACT.Exp).then_inc(S["wkv_exps"], 1)
            act.wait_ge(S["wkv_args"], NC)
            act.activation(arg[:, NC - 1, :, :], arg[:, NC - 1, :, :], ACT.Exp).then_inc(S["wkv_exps"], 1)

            def copy_xT(i, s):
                act.wait_ge(S["moe_xT_mm"], i + 1)
                act.activation(xrT[:, s, :], bank[0][:, 0:P], ACT.Copy).then_inc(S["moe_xT_ready"], 1)

            def gelu(i, s):
                act.wait_ge(S["moe_h_mm"], i + 1)
                for f in range(NF):
                    g = act.activation(hT[:, s, f * P:(f + 1) * P], bank[5 + s][:, f * P:(f + 1) * P], ACT.Gelu,
                                       bias=ew[:, s, 2 * F + f:2 * F + f + 1])
                g.then_inc(S["moe_h_ready"], 1)

            def copy_y(i, s, before):
                act.wait_ge(S["moe_y_mm"], i + 1)
                act.wait_ge(moe_out[s], before * 16)
                act.activation(ye[:, s, :], bank[1][:, 0:C], ACT.Copy).then_inc(S["moe_y_ready"], 1)

            copy_xT(0, 0)
            gelu(0, 0)
            copy_xT(1, 1)
            with act.Fori(0, MT // RING - 1) as r:
                for u in range(RING):
                    i = r * RING + u + 1
                    gelu(i, (u + 1) % RING)
                    copy_xT(i + 1, (u + 2) % RING)
                    copy_y(i - 1, u, r)
            gelu(MT - 2, (MT - 2) % RING)
            copy_xT(MT - 1, (MT - 1) % RING)
            copy_y(MT - 3, (MT - 3) % RING, MT // RING - 1)
            gelu(MT - 1, (MT - 1) % RING)
            copy_y(MT - 2, (MT - 2) % RING, MT // RING - 1)
            copy_y(MT - 1, (MT - 1) % RING, MT // RING - 1)

            for j in range(NC):
                act.wait_ge(S["xT_mm"], NC + j + 1)
                act.activation(xnT[:, 1 + CH * j:1 + CH * (j + 1)], bank[j % 2], ACT.Copy).then_inc(S["xT_ready"], 1)
                if j >= 2:
                    act.wait_ge(mid[0], 48 * (j - 1))
                    act.wait_ge(mid[1], 48 * (j - 1))
                act.wait_ge(S["q_mm"], j + 1)
                act.activation(piece[:, j % 2, 0, 0, :], bank[2], ACT.Copy).then_inc(S["q_split"], 1)
                if j:
                    act.wait_ge(S["norm_mm"], 2 * j)
                act.activation(sq[:, 0, :], bank[2], ACT.Square).then_inc(S["sq_ready"], 1)
                act.wait_ge(S["k2_mm"], j + 1)
                act.activation(piece[:, j % 2, 1, 0, :], bank[3], ACT.Copy).then_inc(S["q_split"], 1)
                act.activation(sq[:, 1, :], bank[3], ACT.Square).then_inc(S["sq_ready"], 1)
                act.wait_ge(S["v2_mm"], j + 1)
                act.activation(v_aug[:, TPC * j:TPC * (j + 1), :, 0:HD],
                               bank[4].rearrange("p (t h d) -> p t h d", t=TPC, h=H), ACT.Copy).then_inc(S["v_aug_ready"], 1)
            for j in range(NC):
                c = slice(CH * j, CH * (j + 1))
                act.wait_ge(S["fk_mm"], j + 1)
                act.activation(buf_a[:, c], bank[7], ACT.Relu).then_inc(S["relu_ready"], 1)
                act.wait_ge(S["fr_mm"], j + 1)
                act.activation(buf_b[:, c], bank[0], ACT.Exp, scale=-1.0).then_inc(S["fe_ready"], 1)
                act.wait_ge(S["fkv_mm"], j + 1)
                act.activation(buf_a[:, c], bank[1], ACT.Copy).then_inc(S["fkv_ready"], 1)
            with act.Fori(0, NQ) as r:
                for u in range(G * NKT):
                    for half in range(2):
                        n = 2 * u + half
                        act.wait_ge(S["scores_mm"], r * (2 * G * NKT) + n + 1)
                        if u >= 4 and half == 0:
                            act.wait_ge(S["pv_mm"], r * (G * NKT) + u - 3)
                        b = 2 * (n % 3)
                        act.activation(probs[:, u % 4, 2 * half:2 * half + 2, :], psum[:, b:b + 2, :], ACT.Exp, scale=SCALE).then_inc(S["exps_done"], 1)

        @block.vector
        def _(dve):
            n = [0]

            def step(ins):
                n[0] += 1
                ins.then_inc(S["dve_step"], 1)

            def settle():
                dve.wait_ge(S["dve_step"], n[0])

            def tile_stats(j):
                for t in range(TPC * j, TPC * j + TPC):
                    step(dve.bn_stats(stats[:, t, :], xs[:, t, :]))
                settle()
                for t in range(TPC * j, TPC * j + TPC):
                    step(dve.bn_aggr(mv[:, t, :], stats[:, t, :]))
                settle()
                g = slice(TPC * j, TPC * j + TPC)
                dve.tensor_scalar(veps[:, g], mv[:, g, 1], EPS, None, ALU.add).then_inc(S["ln_var"], 1)

            def normalise(j, turn):
                dve.wait_ge(S["ln_rstd"], turn * NC + j + 1)
                for t in range(TPC * j, TPC * j + TPC):
                    last = dve.tensor_scalar(xn[:, t, 0:C], xs[:, t, :], mv[:, t, 0:1], rstd[:, t:t + 1], ALU.subtract, ALU.mult)
                last.then_inc(S["xn_ready"], 1)

            step(dve.memset(xnT[:, 0:1], 0.0))
            step(dve.memset(m_run[:, 0:1], NEG))
            step(dve.memset(a_run[:, 0:1], 0.0))
            step(dve.memset(b_run[:, 0:1], 0.0))
            for j in range(NC):
                dve.wait_ge(x_in[j], 16)
                tile_stats(j)
                if j:
                    normalise(j - 1, 0)
            normalise(NC - 1, 0)
            dve.wait_ge(S["decay_exp"], 1)
            step(dve.tensor_scalar(decay[:, :], decay[:, :], -1.0, None, ALU.mult))

            dve.wait_ge(S["router_mm"], 1)
            dve.wait_ge(S["const_in"], 32)
            step(dve.tensor_tensor(score[:, :, :], bank[5][:, 0:NT * E].rearrange("p (t e) -> p t e", e=E),
                                   rb[:, :].unsqueeze(1).to_broadcast([P, NT, E]), ALU.add))
            settle()
            step(dve.tensor_reduce(best[:, :], score[:, :, :], AX.X, ALU.max))
            settle()
            step(dve.tensor_tensor(hot[:, :, :], score[:, :, :], best[:, :].unsqueeze(2).to_broadcast([P, NT, E]), ALU.is_equal))
            settle()
            dve.wait_ge(S["ident_ready"], 1)
            step(dve.tensor_tensor(score[:, :, :], hot[:, :, :], rev[:, :].unsqueeze(1).to_broadcast([P, NT, E]), ALU.mult))
            settle()
            step(dve.tensor_reduce(best[:, :], score[:, :, :], AX.X, ALU.max))
            settle()
            dve.tensor_tensor(hot[:, :, :], rev[:, :].unsqueeze(1).to_broadcast([P, NT, E]),
                              best[:, :].unsqueeze(2).to_broadcast([P, NT, E]), ALU.is_equal).then_inc(S["hot_ready"], 1)
            dve.wait_ge(S["prefix_mm"], 1)
            step(dve.tensor_copy(tot[:, :, :], bank[7][:, 0:NT * E].rearrange("p (t e) -> p e t", e=E)))
            settle()
            flat = "p e t -> p (e t)"
            step(dve.tensor_tensor_scan(cum[:, :, :].rearrange(flat), tot[:, :, :].rearrange(flat), tot[:, :, :].rearrange(flat),
                                        0.0, ALU.add, ALU.max))
            step(dve.tensor_reduce(cnt[:, :], tot[:, :, :], AX.X, ALU.add))
            settle()
            step(dve.tensor_tensor(over[:, :, :], cnt[:, :].unsqueeze(2).to_broadcast([P, E, NT]),
                                   full[:, :].unsqueeze(1).to_broadcast([P, E, NT]), ALU.is_gt))
            step(dve.tensor_tensor(adj[:, :], cnt[:, :], cum[:, :, NT - 1], ALU.subtract))
            settle()
            step(dve.tensor_tensor(cum[:, :, :], cum[:, :, :], tot[:, :, :], ALU.subtract))
            step(dve.tensor_reduce(ntile[:, :], over[:, :, :], AX.X, ALU.add))
            settle()
            step(dve.tensor_tensor_scan(tend[:, :], ntile[:, :], ntile[:, :], 0.0, ALU.add, ALU.max))
            settle()
            step(dve.tensor_tensor(ntile[:, :], tend[:, :], ntile[:, :], ALU.subtract))
            step(dve.tensor_tensor(tge[:, :, :], tidx[:, :].unsqueeze(2).to_broadcast([1, MT, E]),
                                   tend[0:1, :].unsqueeze(1).to_broadcast([1, MT, E]), ALU.is_ge))
            settle()
            step(dve.scalar_tensor_tensor(adj[:, :], ntile[:, :], float(P), adj[:, :], ALU.mult, ALU.add))
            step(dve.tensor_reduce(tef[:, :], tge[:, :, :], AX.X, ALU.add))
            settle()
            step(dve.tensor_tensor(cum[:, :, :], cum[:, :, :], adj[:, :].unsqueeze(2).to_broadcast([P, E, NT]), ALU.add))
            step(dve.tensor_scalar(te[:, :], tef[:, :], float(E - 1), None, ALU.min))
            settle()
            step(dve.tensor_tensor(score[:, :, :], bank[6][:, 0:NT * E].rearrange("p (t e) -> p t e", e=E),
                                   cum[:, :, :].rearrange("p e t -> p t e"), ALU.add))
            settle()
            step(dve.tensor_tensor(score[:, :, :], score[:, :, :], hot[:, :, :], ALU.mult))
            settle()
            step(dve.tensor_reduce(slotf[:, :], score[:, :, :], AX.X, ALU.add))
            settle()
            dve.tensor_copy(slot[:, :], slotf[:, :]).then_inc(S["slots_ready"], 1)

            for j in range(NC):
                c, prev = slice(CH * j, CH * (j + 1)), slice(CH * j + 1, CH * (j + 1) + 1)
                dve.wait_ge(S["k_ready"], j + 1)
                settle()
                step(dve.tensor_tensor_scan(m_run[:, prev], decay[:, 0:1].to_broadcast([P, CH]), kf[:, c],
                                            m_run[:, CH * j:CH * j + 1], ALU.add, ALU.max))
                step(dve.scalar_tensor_tensor(dd[:, c], kf[:, c], vec[:, 1:2], kf[:, c], ALU.add, ALU.bypass)) if False else None
                settle()
                step(dve.scalar_tensor_tensor(dd[:, c], kf[:, c], vec[:, 1:2], m_run[:, c], ALU.add, ALU.subtract))
                step(dve.scalar_tensor_tensor(arg[:, j, 0, :], m_run[:, c], decay[:, 0:1], m_run[:, prev], ALU.add, ALU.subtract))
                step(dve.tensor_tensor(arg[:, j, 1, :], kf[:, c], m_run[:, prev], ALU.subtract))
                settle()
                step(dve.tensor_scalar(arg[:, j, 2, :], dd[:, c], -1.0, 0.0, ALU.mult, ALU.min))
                dve.tensor_scalar(arg[:, j, 3, :], dd[:, c], 0.0, None, ALU.min).then_inc(S["wkv_args"], 1)
            for j in range(NC):
                c, prev = slice(CH * j, CH * (j + 1)), slice(CH * j + 1, CH * (j + 1) + 1)
                dve.wait_ge(S["wkv_exps"], j + 1)
                dve.wait_ge(S["v_ready"], j + 1)
                settle()
                step(dve.tensor_tensor(tmp, arg[:, j, 1, :], vf[:, c], ALU.mult))
                step(dve.tensor_tensor_scan(b_run[:, prev], arg[:, j, 0, :], arg[:, j, 1, :], b_run[:, CH * j:CH * j + 1], ALU.mult, ALU.add))
                settle()
                step(dve.tensor_tensor_scan(a_run[:, prev], arg[:, j, 0, :], tmp, a_run[:, CH * j:CH * j + 1], ALU.mult, ALU.add))
                settle()
                dve.sem_inc(S["wkv_scans"], 1)
                step(dve.tensor_tensor(tmp2, arg[:, j, 2, :], a_run[:, c], ALU.mult))
                dve.wait_ge(S["wkv_pool"], 2 * j + 2)
                dve.wait_ge(S["e_ready"], j + 1)
                settle()
                step(dve.tensor_tensor(arg[:, j, 0, :], arg[:, j, 0, :], arg[:, j, 3, :], ALU.add))
                settle()
                step(dve.scalar_tensor_tensor(arg[:, j, 0, :], ef[:, c], 1.0, arg[:, j, 0, :], ALU.add, ALU.mult))
                step(dve.tensor_tensor(tmp2, tmp2, arg[:, j, 1, :], ALU.add))
                settle()
                step(dve.reciprocal(arg[:, j, 0, :], arg[:, j, 0, :]))
                settle()
                dve.tensor_tensor(buf_a[:, c], tmp2, arg[:, j, 0, :], ALU.mult).then_inc(S["rwkv_ready"], 1)
            for j in range(NC):
                xj = xs[:, TPC * j:TPC * (j + 1), :].rearrange("p n c -> p (n c)")
                dve.wait_ge(S["attn_mm"], j + 1)
                step(dve.tensor_tensor(xj, xj, bank[4 + j], ALU.add))
            dve.wait_ge(S["moe_in"], 16)
            for j in range(NC):
                xj = xs[:, TPC * j:TPC * (j + 1), :].rearrange("p n c -> p (n c)")
                settle()
                step(dve.tensor_tensor(xj, xj, buf_b[:, CH * j:CH * (j + 1)], ALU.add))
                settle()
                dve.sem_inc(S["x1_ready"], 1)
                tile_stats(j)
                if j:
                    normalise(j - 1, 1)
            normalise(NC - 1, 1)
            for j in range(NC):
                if j >= 2:
                    dve.wait_ge(mid[0], 48 * (j - 1))
                    dve.wait_ge(mid[1], 48 * (j - 1))
                for s in range(2):
                    dve.wait_ge(S["sq_ready"], 2 * j + s + 1)
                    p = piece[:, j % 2, s]
                    settle()
                    step(dve.tensor_tensor(left, bank[2 + s], p[:, 0, :], ALU.subtract))
                    settle()
                    step(dve.tensor_copy(p[:, 1, :], left))
                    settle()
                    step(dve.tensor_tensor(p[:, 2, :], left, p[:, 1, :], ALU.subtract))
                    settle()
                    dve.sem_inc(S["piece_ready"], 1)
                dve.wait_ge(S["norm_mm"], 2 * j + 1)
                step(dve.tensor_copy(norm[:, CH * j:CH * (j + 1)], bank[5][0:H, :]))
                step(dve.tensor_reduce(nmax[:, 0, j:j + 1], bank[5][0:H, :], AX.X, ALU.max))
                dve.wait_ge(S["norm_mm"], 2 * j + 2)
                dve.tensor_reduce(nmax[:, 1, j:j + 1], bank[6][0:H, :], AX.X, ALU.max).then_inc(S["norms_read"], 1)
            dve.wait_ge(S["norms_read"], NC)
            settle()
            step(dve.tensor_reduce(nbest[:, 0:2], nmax[:, :, :], AX.X, ALU.max))
            settle()
            dve.tensor_tensor(nbest[:, 2:3], nbest[:, 0:1], nbest[:, 1:2], ALU.add).then_inc(S["stack_set"], 1)
            step(dve.tensor_scalar(norm, norm, nbest[:, 1:2], -0.5, ALU.add, ALU.mult))
            dve.wait_ge(S["flag_mm"], 1)
            step(dve.tensor_reduce(flagf[:, :], bank[6][0:1, 0:H], AX.X, ALU.max))
            settle()
            dve.tensor_scalar(flag[:, :], flagf[:, :], SAFE, None, ALU.is_gt).then_inc(S["flag_ready"], 1)
            dve.wait_ge(S["flag_ready"], 1)
            wide = dve.value_load(flag[0:1, 0:1], min_val=0, max_val=1)
            with dve.If(wide):
                with dve.Fori(0, H // 2) as g:
                    for half in range(2):
                        with dve.Fori(0, NT) as t:
                            dve.wait_ge(S["gmax_mm"], g * (2 * NT) + half * NT + t + 1)
                            dve.tensor_reduce(top[:, bass.ds(t, 1), bass.ds(g * 2 + half, 1)].rearrange("p a b -> p (a b)"),
                                              psum[:, 0:NC, :], AX.XY, ALU.max).then_inc(S["gmax_read"], 1)
                dve.wait_ge(S["gmax_turned"], 1)
                dve.tensor_scalar(norm, psum[0:H, 0:NC, :].rearrange("h a b -> h (a b)"), -1.0, None, ALU.mult).then_inc(S["gmax_read"], 1)
                dve.wait_ge(S["gmax_read"], H * NT + 1)
            settle()
            step(dve.tensor_copy(shiftp[:, 0, :], norm))
            settle()
            step(dve.tensor_tensor(shiftp[:, 1, :], norm, shiftp[:, 0, :], ALU.subtract))
            settle()
            dve.sem_inc(S["shift_ready"], 1)
            dve.wait_ge(S["relu_ready"], NC)
            dve.memset(psum[:, 6:8, :], 0.0).then_inc(S["acc_zeroed"], 1)
            for j in range(NC):
                c = slice(CH * j, CH * (j + 1))
                dve.wait_ge(S["fe_ready"], j + 1)
                step(dve.tensor_scalar(buf_b[:, c], buf_b[:, c], 1.0, None, ALU.add))
                settle()
                step(dve.reciprocal(buf_b[:, c], buf_b[:, c]))
                dve.wait_ge(S["fkv_ready"], j + 1)
                settle()
                dve.tensor_tensor(buf_b[:, c], buf_b[:, c], buf_a[:, c], ALU.mult).then_inc(S["z_ready"], 1)
            base = n[0]
            with dve.Fori(0, NQ) as r:
                for g in range(G):
                    dve.wait_ge(S["pv_mm"], r * (G * NKT) + NKT * (g + 1))
                    dve.wait_ge(y_packed[g % 2], r * (16 * HG * 2) + 16 * HG * (g // 2))
                    dve.tensor_copy(y_g[:, g % 2, :], bank[6 + g % 2]).then_inc(S["acc_free"], 1)
                    dve.wait_ge(S["acc_free"], r * G + g + 1)
                    k = r * (3 * G) + (base + 3 * g)
                    dve.wait_ge(S["dve_step"], k)
                    dve.sem_inc(S["shuffle_turn"], 1)
                    dve.stream_shuffle(y_den[:, :], y_g[:, g % 2, :], [HD] * 32).then_inc(S["dve_step"], 1)
                    dve.wait_ge(S["dve_step"], k + 1)
                    dve.reciprocal(y_den[:, :], y_den[:, :]).then_inc(S["dve_step"], 1)
                    dve.wait_ge(S["dve_step"], k + 2)
                    dve.tensor_tensor(y_g[:, g % 2, :], y_g[:, g % 2, :], y_den[:, :], ALU.mult).then_inc(S["dve_step"], 1)
                    dve.wait_ge(S["dve_step"], k + 3)
                    dve.sem_inc(S["y_ready"], 1)
            for j in range(NC):
                xj = xs[:, TPC * j:TPC * (j + 1), :].rearrange("p n c -> p (n c)")
                dve.wait_ge(S["proj_mm"], j + 1)
                dve.tensor_tensor(xj, xj, bank[j], ALU.add).then_inc(S["x1_ready"], 1)

        @block.tensor
        def _(pe):
            pe.wait_ge(S["ident_ready"], 1)

            def transposes(j, turn):
                pe.wait_ge(S["xn_ready"], turn * NC + j + 1)
                if j >= 2:
                    pe.wait_ge(S["xT_ready"], turn * NC + j - 1)
                for t in range(TPC):
                    mm = pe.transpose(bank[j % 2][:, P * t:P * (t + 1)], xn[:, TPC * j + t, 0:C], ident[:, :])
                mm.then_inc(S["xT_mm"], 1)

            def router(j):
                pe.wait_ge(S["xT_ready"], j + 1)
                for t in range(TPC * j, TPC * (j + 1)):
                    mm = pe.matmul(bank[5][:, E * t:E * (t + 1)], xnT[:, 1 + P * t:1 + P * (t + 1)], rw[:, :], start=True, stop=True)
                return mm

            for j in range(NC):
                transposes(j, 0)
                if j == 0:
                    pe.wait_ge(S["const_in"], 32)
                    pe.wait_ge(S["dve_step"], 1)
                mm = router(j)
            mm.then_inc(S["router_mm"], 1)

            def mixed(b, w, j, done, freed):
                if j:
                    pe.wait_ge(freed, j)
                pe.matmul(bank[b], mix[:, w, 0, :], xnT[:, 1 + CH * j:1 + CH * (j + 1)], start=True, stop=False)
                pe.matmul(bank[b], mix[:, w, 1, :], xnT[:, CH * j:CH * (j + 1)], start=False, stop=True).then_inc(done, 1)

            pe.wait_ge(S["mix_ready"], 3)
            for j in range(NC):
                mixed(2, 0, j, S["k_mm"], S["k_ready"])
                mixed(3, 1, j, S["v_mm"], S["v_ready"])
                mixed(4, 2, j, S["r_mm"], S["e_ready"])
                if j == 0:
                    pe.wait_ge(S["hot_ready"], 1)
                    hot_f = hot[:, :, :].rearrange("p t e -> p (t e)")
                    pe.matmul(bank[6][:, 0:NT * E], before[:, :], hot_f, start=True, stop=True)
                    pe.matmul(bank[7][:, 0:NT * E], ones[:, :], hot_f, start=True, stop=True).then_inc(S["prefix_mm"], 1)

            def turn_x(i, s, fills, free):
                pe.wait_ge(slot_in[s], fills * 48)
                if free:
                    pe.wait_ge(S["moe_xT_ready"], i)
                pe.transpose(bank[0][:, 0:P], xr[:, s, 0:C], ident[:, :]).then_inc(S["moe_xT_mm"], 1)

            def up(i, s):
                pe.wait_ge(S["moe_xT_ready"], i + 1)
                for f in range(NF):
                    mm = pe.matmul(bank[5 + s][:, P * f:P * (f + 1)], ew[:, s, P * f:P * (f + 1)], xrT[:, s, :], start=True, stop=True)
                mm.then_inc(S["moe_h_mm"], 1)

            def down(i, s, free):
                pe.wait_ge(S["moe_h_ready"], i + 1)
                if free:
                    pe.wait_ge(S["moe_y_ready"], i)
                for f in range(NF):
                    pe.matmul(bank[1][:, 0:C], hT[:, s, P * f:P * (f + 1)], ew[:, s, F + C * f:F + C * (f + 1)], start=(f == 0), stop=False)
                pe.matmul(bank[1][:, 0:C], ones[0:1, :], eb2[0:1, s, :], start=False, stop=True).then_inc(S["moe_y_mm"], 1)

            turn_x(0, 0, 1, False)
            pe.wait_ge(S["slots_ready"], 1)
            up(0, 0)
            turn_x(1, 1, 1, True)
            with pe.Fori(0, MT // RING - 1) as r:
                for u in range(RING):
                    i = r * RING + u + 1
                    up(i, (u + 1) % RING)
                    turn_x(i + 1, (u + 2) % RING, r + 1 + (u + 2) // RING, True)
                    down(i - 1, u, True)
            i = MT - 2
            up(i, i % RING)
            turn_x(i + 1, (i + 1) % RING, MT // RING, True)
            down(i - 1, (i - 1) % RING, True)
            up(i + 1, (i + 1) % RING)
            down(i, i % RING, True)
            down(i + 1, (i + 1) % RING, True)
            for j in range(NC):
                pe.wait_ge(S["rwkv_ready"], j + 1)
                for t in range(TPC):
                    k = TPC * j + t
                    mm = pe.matmul(bank[4 + j][:, P * t:P * (t + 1)], buf_a[:, P * k:P * (k + 1)], wts[:, 3, :], start=True, stop=True)
                mm.then_inc(S["attn_mm"], 1)


            pe.wait_ge(S["wq_in"], 32)

            def norms(j):
                for s in range(2):
                    pe.wait_ge(S["sq_ready"], 2 * j + s + 1)
                    if j and s == 0:
                        pe.wait_ge(S["norms_read"], j)
                    pe.matmul(bank[5 + s][0:H, :], headsel[:, :], sq[:, s, :], start=True, stop=True).then_inc(S["norm_mm"], 1)

            for j in range(NC):
                transposes(j, 1)
                pe.wait_ge(S["xT_ready"], NC + j + 1)
                c = slice(1 + CH * j, 1 + CH * (j + 1))
                if j:
                    pe.wait_ge(S["piece_ready"], 2 * j)
                pe.matmul(bank[2], wqkv[:, 0:C], xnT[:, c], start=True, stop=True).then_inc(S["q_mm"], 1)
                pe.matmul(bank[3], wqkv[:, C:2 * C], xnT[:, c], start=True, stop=True).then_inc(S["k2_mm"], 1)
                if j:
                    pe.wait_ge(S["v_aug_ready"], j)
                for t in range(TPC):
                    k = TPC * j + t
                    mm = pe.matmul(bank[4][:, P * t:P * (t + 1)], xnT[:, 1 + P * k:1 + P * (k + 1)], wqkv[:, 2 * C:3 * C], start=True, stop=True)
                mm.then_inc(S["v2_mm"], 1)
                norms(j)
            pe.wait_ge(S["stack_set"], 1)
            pe.transpose(bank[6][0:1, 0:H], nbest[:, 2:3], ident[0:H, 0:H]).then_inc(S["flag_mm"], 1)
            pe.wait_ge(S["flag_ready"], 1)
            wide = pe.value_load(flag[0:1, 0:1], min_val=0, max_val=1)
            with pe.If(wide):
                pe.wait_ge(stack_in, 16 * 4 * NC)
                with pe.Fori(0, H // 2) as g:
                    for half in range(2):
                        with pe.Fori(0, NT) as t:
                            pe.wait_ge(S["gmax_read"], g * (2 * NT) + half * NT + t)
                            for b in range(NC):
                                mm = pe.matmul(bank[b], q_stack[:, bass.ds(g, 1), bass.ds(t * P, P)].rearrange("p a b -> p (a b)"),
                                               k_stack[:, bass.ds(g * 2 + half, 1), CH * b:CH * (b + 1)].rearrange("p a b -> p (a b)"),
                                               start=True, stop=True)
                            mm.then_inc(S["gmax_mm"], 1)
                pe.wait_ge(S["gmax_read"], H * NT)
                for t in range(NT):
                    mm = pe.transpose(bank[t // TPC][0:H, P * (t % TPC):P * (t % TPC + 1)], top[:, t, :], ident[:, :])
                mm.then_inc(S["gmax_turned"], 1)
                pe.wait_ge(S["gmax_read"], H * NT + 1)
            for j in range(NC):
                for w, b, done, freed in ((4, 7, "fk_mm", "relu_ready"), (3, 0, "fr_mm", "fe_ready")):
                    if j:
                        pe.wait_ge(S[freed], j)
                    pe.matmul(bank[b], mix[:, w, 0, :], xnT[:, 1 + CH * j:1 + CH * (j + 1)], start=True, stop=False)
                    pe.matmul(bank[b], mix[:, w, 1, :], xnT[:, CH * j:CH * (j + 1)], start=False, stop=True).then_inc(S[done], 1)
                pe.wait_ge(S["kact_ready"], j + 1)
                if j:
                    pe.wait_ge(S["fkv_ready"], j)
                pe.matmul(bank[1], wts[:, 6, :], buf_a[:, CH * j:CH * (j + 1)], start=True, stop=True).then_inc(S["fkv_mm"], 1)
            pe.wait_ge(S["fkv_ready"], NC)
            pe.wait_ge(S["fe_ready"], NC)
            pe.wait_ge(stack_in, 16 * 4 * NC)
            pe.wait_ge(S["shift_in"], 32)
            pe.wait_ge(S["acc_zeroed"], 1)

            def attend(r, u):
                g, kt = divmod(u, NKT)
                pe.wait_ge(S["exps_done"], r * (2 * G * NKT) + 2 * (u + 1))
                if kt == 0:
                    pe.wait_ge(S["acc_free"], r * G + (g - 1 if g else 0))
                for h in range(HG):
                    mm = pe.matmul(bank[6 + g % 2][32 * h:32 * h + HD + 1, :], v_aug[:, kt, HG * g + h, :], probs[:, u % 4, h, :],
                                   start=(kt == 0), stop=(kt == NKT - 1))
                mm.then_inc(S["pv_mm"], 1)

            with pe.Fori(0, NQ) as r:
                for u in range(G * NKT):
                    g, kt = divmod(u, NKT)
                    for half in range(2):
                        n = 2 * u + half
                        if n >= 3:
                            pe.wait_ge(S["exps_done"], r * (2 * G * NKT) + n - 2)
                        for h in range(2):
                            hh = HG * g + 2 * half + h
                            mm = pe.matmul(bank[2 * (n % 3) + h], k_stack[:, hh, P * kt:P * (kt + 1)],
                                           q_stack[:, hh // 2, bass.ds(r * CH, CH)], start=True, stop=True)
                        mm.then_inc(S["scores_mm"], 1)
                    if u:
                        attend(r, u - 1)
                attend(r, G * NKT - 1)
            for s in range(2):
                pe.wait_ge(y_packed[s], 16 * HG * NQ * 2)
            pe.wait_ge(S["z_ready"], NC)
            for j in range(NC):
                for t in range(TPC):
                    k = TPC * j + t
                    pe.matmul(bank[j][:, P * t:P * (t + 1)], yT[:, P * k:P * (k + 1)], wo1[:, :], start=True, stop=False)
                    mm = pe.matmul(bank[j][:, P * t:P * (t + 1)], buf_b[:, P * k:P * (k + 1)], ident[:, :], start=False, stop=True)
                mm.then_inc(S["proj_mm"], 1)


_OUTS = [((1, 2048, 128), "float32")]


def kernel(**inputs):
    import numpy as np
    import concourse.bacc as bacc
    from concourse import mybir as mb
    from concourse.bass_utils import run_bass_kernel_spmd as run

    a = {k: np.asarray(v) for k, v in inputs.items()}
    flat = lambda v: np.reshape(v, (-1,))
    vecs = np.stack([flat(a[k]) for k in ("L0_attn_W", "L0_attn_U", "L0_attn_time_mix_k", "L0_attn_time_mix_v",
                                          "L0_attn_time_mix_r", "L1_ffn_mu_r", "L1_ffn_mu_k")], axis=1)
    w_t = np.concatenate([a[k].T for k in ("L0_attn_Wk", "L0_attn_Wv", "L0_attn_Wr", "L0_attn_Wo",
                                           "L1_ffn_W_r", "L1_ffn_W_k", "L1_ffn_W_v")], axis=1)
    w1, b1, w2 = a["L0_ffn_w1"], a["L0_ffn_b1"], a["L0_ffn_w2"]
    e, f, h = w2.shape
    w2r = np.transpose(np.reshape(w2, (e, f // 128, 128, h)), (0, 2, 1, 3)).reshape(e, 128, f // 128 * h)
    b1r = np.transpose(np.reshape(b1, (e, f // 128, 128)), (0, 2, 1))
    expert_w = np.concatenate([w1, w2r, b1r], axis=2)
    arrays = {"in_x": a["L0_attn_x"], "in_vecs": vecs, "in_w_t": w_t, "in_router_w": a["L0_ffn_wr"],
              "in_router_b": a["L0_ffn_br"], "in_expert_w": expert_w, "in_expert_b2": a["L0_ffn_b2"],
              "in_w_qkv": a["L1_attn_w_qkv"], "in_w_out": a["L1_attn_w_out"]}
    arrays = {k: np.ascontiguousarray(v) for k, v in arrays.items()}
    nc = bacc.Bacc("TRN2", target_bir_lowering=False, num_devices=1)
    args = [nc.dram_tensor(k, v.shape, mb.dt.from_np(v.dtype), kind="ExternalInput").ap() for k, v in arrays.items()]
    for i, (shape, dtype) in enumerate(_OUTS):
        args.append(nc.dram_tensor(f"out_{i}", shape, mb.dt.from_np(np.dtype(dtype)), kind="ExternalOutput").ap())
    two_layer_kernel(nc, *args)
    r = run(nc, [arrays], core_ids=[0])
    return r.results[0]["out_0"]
```

```python
import concourse.bass as bass
from concourse import mybir
from contextlib import ExitStack


def two_layer_kernel(nc: bass.Bass, x, vecs, w_t, router_w, router_b, expert_w1, expert_w2, expert_b1, expert_b2, w_qkv, w_out, out):
    fp32, bf16 = mybir.dt.float32, mybir.dt.bfloat16
    i32, u32 = mybir.dt.int32, mybir.dt.uint32
    ALU, ACT, AX = mybir.AluOpType, mybir.ActivationFunctionType, mybir.AxisListType

    P = 128
    T, C = x.shape[1], x.shape[2]
    NT = T // P
    CH = 512
    NC = T // CH
    TPC = CH // P
    E = router_w.shape[1]
    F = expert_w1.shape[2]
    NF = F // P
    RING = 3
    MT = NT + E
    assert MT % RING == 0
    ROWS = MT * P
    XW = C + 4
    H, HD = 16, 8
    G, HG = 4, 4
    NKT = T // P
    NQ = T // CH
    assert NQ == NC == G == 4
    SCALE = float(HD) ** -0.5
    NEG = -1e38
    EPS = 1e-5
    SAFE = 226.0

    x_t = x.rearrange("a (n p) c -> p (a n) c", p=P)
    out_t = out.rearrange("a (n p) c -> p (a n) c", p=P)
    routed = nc.dram_tensor("routed", (ROWS, XW), fp32, kind="Internal").ap()
    moe = nc.dram_tensor("moe", (T, C), fp32, kind="Internal").ap()
    moe_t = moe.rearrange("(n p) c -> p n c", p=P)
    NB = 6
    stacked = nc.dram_tensor("stacked", (2, C, NB, T), bf16, kind="Internal").ap()
    shifts = nc.dram_tensor("shifts", (H, 2, T), bf16, kind="Internal").ap()
    ROW0 = 8

    ctx = ExitStack()
    with ctx:
        def sb(name, shape, dt=fp32):
            return ctx.enter_context(nc.sbuf_tensor(name, shape, dt))

        def sem(name):
            return ctx.enter_context(nc.semaphore(name))

        psum = ctx.enter_context(nc.psum_tensor("psum", [P, 8, CH], fp32))
        bank = [psum[:, i, :] for i in range(8)]

        xs = sb("xs", [P, NT, C])
        xn = sb("xn", [P, NT, XW])
        xnT = sb("xnT", [P, T + 1])
        buf_a = sb("buf_a", [P, T])
        buf_b = sb("buf_b", [P, T])
        ident = sb("ident", [P, P])
        ones = sb("ones", [P, P])
        before = sb("before", [P, P])
        vec = sb("vec", [P, 7])
        wts = sb("wts", [P, 7, C])
        mix = sb("mix", [P, 5, 2, C])
        wqkv = sb("wqkv", [P, 3 * C])
        wo1 = sb("wo1", [P, C])
        stats = sb("stats", [P, NT, 6])
        mv = sb("mv", [P, NT, 2])
        veps = sb("veps", [P, NT])
        halves = sb("halves", [P, NT])
        rstd = sb("rstd", [P, NT])
        pad = sb("pad", [P, XW])

        k_stack = sb("k_stack", [P, H, T], bf16)
        q_stack = sb("q_stack", [P, H // 2, T], bf16)
        probs = sb("probs", [P, 4, HG, CH])
        v_aug = sb("v_aug", [P, NKT, H, HD + 1])
        yT = xn[:, :, :].rearrange("p n c -> p (n c)")[:, 0:T]
        y_g = sb("y_g", [P, 2, CH])
        y_den = sb("y_den", [P, CH])

        QZ = 5632
        ks32 = k_stack[:, :, :].rearrange("p h t -> p (h t)").bitcast(fp32)
        arg = ks32[:, 0:4 * T].rearrange("p (j a t) -> p j a t", j=NC, a=4)
        kf, vf, ef, dd = (ks32[:, (4 + i) * T:(5 + i) * T] for i in range(4))
        pr32 = probs[:, :, :, :].rearrange("p a h t -> p (a h t)")
        m_run, a_run, b_run = (pr32[:, i * (T + 1):(i + 1) * (T + 1)] for i in range(3))
        tmp = pr32[:, 3 * (T + 1):3 * (T + 1) + CH]
        tmp2 = pr32[:, 3 * (T + 1) + CH:3 * (T + 1) + 2 * CH]
        qs32 = q_stack[:, :, :].rearrange("p h t -> p (h t)").bitcast(fp32)
        w2 = qs32[:, 0:E * F]
        w1 = qs32[:, E * F:E * F + RING * F].rearrange("p (s n) -> p s n", s=RING)
        xr = buf_b[:, 0:RING * C].rearrange("p (s n) -> p s n", s=RING)
        ye = buf_b[:, RING * C:2 * RING * C].rearrange("p (s n) -> p s n", s=RING)
        row_id = buf_b[:, 2 * RING * C:2 * RING * C + MT].bitcast(u32)
        va32 = v_aug[:, :, :, :].rearrange("p n h d -> p (n h d)")
        hT = va32[:, 0:RING * F].rearrange("p (s n) -> p s n", s=RING)
        xrT = va32[:, RING * F:RING * (F + P)].rearrange("p (s n) -> p s n", s=RING)
        b1 = sb("b1", [P, E * NF])
        b2 = sb("b2", [1, E * C])

        rb = sb("rb", [P, E])
        rw = sb("rw", [P, E])
        score = sb("score", [P, NT, E])
        best = sb("best", [P, NT])
        rev = sb("rev", [P, E])
        hot = sb("hot", [P, NT, E])
        tot = sb("tot", [P, E, NT])
        cum = sb("cum", [P, E, NT])
        cnt = sb("cnt", [P, E])
        full = sb("full", [P, NT])
        over = sb("over", [P, E, NT])
        ntile = sb("ntile", [P, E])
        tend = sb("tend", [P, E])
        adj = sb("adj", [P, E])
        slotf = sb("slotf", [P, NT])
        slot = sb("slot", [P, NT], u32)
        tidx = sb("tidx", [1, MT])
        tge = sb("tge", [1, MT, E])
        tef = sb("tef", [1, MT])
        te = sb("te", [1, MT], i32)
        decay = sb("decay", [P, 1])

        at = [0]

        def ppart(words):
            at[0] += words
            return pr32[:, at[0] - words:at[0]]

        piece = ppart(4 * 3 * CH // 2).bitcast(bf16).rearrange("p (r s k t) -> p r s k t", r=2, s=2, k=3)
        left = ppart(2 * CH).rearrange("p (s t) -> p s t", s=2)
        sq = ppart(2 * CH).bitcast(bf16).rearrange("p (r s t) -> p r s t", r=2, s=2)
        top = ppart(NT * H).rearrange("p (n h) -> p n h", n=NT)
        norm = ppart(T)[0:H, :]
        assert at[0] <= pr32.shape[1]
        shiftp = xn[:, :, :].rearrange("p n c -> p (n c)")[0:H, 0:T].bitcast(bf16).rearrange("h (k t) -> h k t", k=2)
        headsel = sb("headsel", [P, H], bf16)
        nmax = sb("nmax", [H, 2, NC])
        nbest = sb("nbest", [H, 3])
        flagf = sb("flagf", [1, 1])
        flag = sb("flag", [1, 1], i32)

        names = """vec_in wts_in wq_in const_in routed_padded pool_step dve_step ident_ready decay_exp mix_ready ln_var ln_rstd xn_ready
            xT_mm xT_ready router_mm hot_ready prefix_mm slots_ready k_mm v_mm r_mm k_ready v_ready e_ready
            wkv_args wkv_exps rwkv_ready scattered moe_xT_mm moe_xT_ready moe_h_mm moe_h_ready
            moe_y_mm moe_y_ready shuffle_turn moe_in experts_in pad_ready v_ones ids_in attn_mm x1_ready
            act_step q_mm k2_mm v2_mm q_split norm_mm norms_read flag_mm flag_ready v_aug_ready k_zeroed q_zeroed
            middle_ready norm_ready piece_ready shift_ready shift_mid shift_in sq_ready gmax_mm gmax_read gmax_turned stack_set
            fk_mm fr_mm fkv_mm relu_ready kact_ready fe_ready fkv_ready z_ready
            scores_mm exps_done pv_mm acc_zeroed acc_free y_ready proj_mm""".split()
        S = {n: sem(n) for n in names}
        x_in = [sem(f"x_in{j}") for j in range(NC)]
        w1_in = [sem(f"w1_in{s}") for s in range(RING)]
        rows_in = [sem(f"rows_in{s}") for s in range(RING)]
        moe_out = [sem(f"moe_out{s}") for s in range(RING)]
        q_mid = [sem(f"q_mid{j}") for j in range(NC)]
        k_mid = [sem(f"k_mid{j}") for j in range(NC)]
        stack_in, q_in, q_all_in = sem("stack_in"), sem("q_in"), sem("q_all_in")
        y_packed = [sem(f"y_packed{i}") for i in range(2)]
        done_out = sem("done_out")
        block = ctx.enter_context(nc.Block())

        @block.sync
        def _(sp):
            for j in range(NC):
                sp.dma_start(xs[:, TPC * j:TPC * (j + 1), :], x_t[:, TPC * j:TPC * (j + 1), :]).then_inc(x_in[j], 16)
            sp.dma_start(rw[:, :], router_w).then_inc(S["const_in"], 16)
            sp.dma_start(rb[:, :], router_b.partition_broadcast(P)).then_inc(S["const_in"], 16)
            sp.dma_start(vec[:, :], vecs).then_inc(S["vec_in"], 16)
            sp.dma_start(wts[:, :, :], w_t.rearrange("p (m n) -> p m n", m=7)).then_inc(S["wts_in"], 16)
            sp.wait_ge(S["pad_ready"], 1)
            rt = routed.rearrange("(m p) c -> p m c", p=P)
            sp.dma_start(rt, pad[:, :].unsqueeze(1).to_broadcast([P, MT, XW])).then_inc(S["routed_padded"], 16)
            sp.dma_start(w2.rearrange("p (e n) -> p e n", e=E), expert_w2.rearrange("e p n -> p e n")).then_inc(S["experts_in"], 16)
            sp.dma_start(b1[:, :], expert_b1).then_inc(S["experts_in"], 16)
            sp.dma_start(b2[:, :], expert_b2).then_inc(S["experts_in"], 16)
            sp.dma_start(wqkv[:, :], w_qkv).then_inc(S["wq_in"], 16)
            sp.dma_start(wo1[:, :], w_out).then_inc(S["wq_in"], 16)
            def load_w1(i, s):
                e = sp.value_load(te[0:1, bass.ds(i, 1)], min_val=0, max_val=E - 1)
                sp.dma_start(w1[:, s, :], expert_w1[bass.ds(e, 1), :, :].rearrange("a p n -> p (a n)")).then_inc(w1_in[s], 16)

            sp.wait_ge(S["slots_ready"], 1)
            for s in range(RING):
                load_w1(s, s)
            def load_rows(i, s):
                sp.dma_start(xr[:, s, :], routed[bass.ds(i * P, P), 0:C]).then_inc(rows_in[s], 16)

            sp.wait_ge(S["scattered"], 16 * NT)
            for s in range(RING):
                load_rows(s, s)
            with nc.allow_non_contiguous_dma(reason="one word of each row"):
                sp.dma_start(row_id, rt[:, :, C].bitcast(u32)).then_inc(S["ids_in"], 16)
            with sp.Fori(0, MT // RING - 1) as r:
                for s in range(RING):
                    sp.wait_ge(S["moe_h_mm"], r * RING + s + 1)
                    load_rows(r * RING + RING + s, s)
                    load_w1(r * RING + RING + s, s)
            sp.wait_ge(S["k_zeroed"], 1)
            for half in range(2):
                one = k_stack[64 * half:64 * half + 2, half:half + 1, :]
                sp.dma_start(k_stack[64 * half:64 * half + 2, half + 2:H:2, :], one.to_broadcast([2, H // 2 - 1, T])).then_inc(stack_in, 16)
            for s in range(RING):
                sp.wait_ge(moe_out[s], 16 * (MT // RING))
            sp.dma_start(buf_b.rearrange("p (n c) -> p n c", n=NT), moe_t).then_inc(S["moe_in"], 16)
            def load_stack(s, c, done):
                for half in range(2):
                    rows = slice(64 * half + ROW0, 64 * half + ROW0 + NB * HD)
                    src = stacked_rows[s][half][:, :, c]
                    dst = q_stack[rows, :, c] if s == 0 else k_stack[rows, half:H:2, c]
                    sp.dma_start(dst, src).then_inc(done, 16)

            stacked_rows = [[stacked[s].rearrange("(g a d) b t -> a (d b) g t", a=2, d=HD)[half] for half in range(2)] for s in range(2)]
            for j in range(NC):
                c = slice(CH * j, CH * (j + 1))
                p = piece[:, j % 2]
                sp.wait_ge(S["piece_ready"], 2 * j + 2)
                for b, m in ((0, 3), (3, 2), (5, 1)):
                    sp.dma_start(stacked[1, :, b:b + m, c], p[:, 1, 0:m, :]).then_inc(k_mid[j], 16)
                for k, b, m in ((0, 0, 3), (1, 3, 2), (2, 5, 1)):
                    sp.dma_start(stacked[0, :, b:b + m, c], p[:, 0, k:k + 1, :].to_broadcast([P, m, CH])).then_inc(q_mid[j], 16)
                sp.wait_ge(k_mid[j], 48)
                load_stack(1, c, stack_in)
                if j == 0:
                    sp.wait_ge(S["q_zeroed"], 2)
                    sp.wait_ge(q_mid[j], 48)
                    load_stack(0, c, q_in)
            for j in range(1, NC):
                sp.wait_ge(q_mid[j], 48)
            sp.wait_ge(S["flag_ready"], 1)
            wide = sp.value_load(flag[0:1, 0:1], min_val=0, max_val=1)
            with sp.If(wide):
                for j in range(1, NC):
                    load_stack(0, slice(CH * j, CH * (j + 1)), q_all_in)
            sp.wait_ge(S["shift_ready"], 1)
            sp.dma_start(shifts, shiftp).then_inc(S["shift_mid"], 16)
            sp.wait_ge(S["shift_mid"], 16)
            for half in range(2):
                sp.dma_start(q_stack[64 * half:64 * half + 2, :, :],
                             shifts.rearrange("(g a) k t -> a k g t", a=2)[half]).then_inc(S["shift_in"], 16)
            for s in range(2):
                sp.sem_inc(y_packed[s], 16)
            def pack(r, g):
                sp.wait_ge(S["y_ready"], r * G + g + 1)
                for h in range(HG):
                    sp.dma_start(yT[32 * g + HD * h:32 * g + HD * (h + 1), bass.ds(r * CH, CH)],
                                 y_g[32 * h:32 * h + HD, g % 2, :]).then_inc(y_packed[g % 2], 16)

            def store(j):
                sp.wait_ge(S["x1_ready"], NC + j + 1)
                sp.dma_start(out_t[:, TPC * j:TPC * (j + 1), :], xs[:, TPC * j:TPC * (j + 1), :]).then_inc(done_out, 16)

            with sp.Fori(0, NQ - 1) as r:
                sp.wait_ge(q_in, r * 32 + 32)
                load_stack(0, bass.ds(r * CH + CH, CH), q_in)
                for g in range(G):
                    pack(r, g)
            pack(NQ - 1, 0)
            pack(NQ - 1, 1)
            store(0)
            store(1)
            pack(NQ - 1, 2)
            store(2)
            pack(NQ - 1, 3)
            store(3)
            sp.wait_ge(done_out, 16 * NC)

        @block.gpsimd
        def _(pool):
            n = [0]

            def step(ins):
                n[0] += 1
                ins.then_inc(S["pool_step"], 1)

            def settle():
                pool.wait_ge(S["pool_step"], n[0])

            step(pool.memset(pad[:, :], 0.0))
            settle()
            step(pool.memset(pad[:, C:C + 1].bitcast(i32), T))
            settle()
            pool.sem_inc(S["pad_ready"], 1)
            step(pool.memset(ones[:, :], 1.0))
            step(pool.memset(halves[:, :], -0.5))
            step(pool.iota(xn[:, :, C:C + 1].bitcast(i32), pattern=[[P, NT]], base=0, channel_multiplier=1))
            step(pool.iota(rev[:, :], pattern=[[-1, E]], base=E, channel_multiplier=0, allow_small_or_imprecise_dtypes=True))
            step(pool.iota(full[:, :], pattern=[[P, NT]], base=0, channel_multiplier=0, allow_small_or_imprecise_dtypes=True))
            step(pool.iota(tidx[:, :], pattern=[[1, MT]], base=0, channel_multiplier=0, allow_small_or_imprecise_dtypes=True))
            step(pool.memset(xn[:, :, C + 1:XW], 0.0))
            settle()
            step(pool.affine_select(out=ident[:, :], in_=ones[:, :], compare_op=ALU.is_equal, fill=0.0,
                                    base=0, pattern=[[-1, P]], channel_multiplier=1))
            step(pool.affine_select(out=before[:, :], in_=ones[:, :], compare_op=ALU.is_gt, fill=0.0,
                                    base=0, pattern=[[1, P]], channel_multiplier=-1))
            settle()
            pool.sem_inc(S["ident_ready"], 1)
            step(pool.affine_select(out=headsel[:, :], in_=ones[:, 0:H], compare_op=ALU.is_ge, fill=0.0,
                                    base=0, pattern=[[-HD, H]], channel_multiplier=1))
            settle()
            step(pool.affine_select(out=headsel[:, :], in_=headsel[:, :], compare_op=ALU.is_ge, fill=0.0,
                                    base=HD - 1, pattern=[[HD, H]], channel_multiplier=-1))

            def rsqrt(j):
                pool.wait_ge(S["ln_var"], j + 1)
                g = slice(TPC * (j % NC), TPC * (j % NC) + TPC)
                pool.tensor_tensor(rstd[:, g], veps[:, g], halves[:, g], ALU.pow).then_inc(S["ln_rstd"], 1)

            def mix_weight(j, w, v):
                step(pool.tensor_scalar(mix[:, j, 0, :], wts[:, w, :], vec[:, v:v + 1], None, ALU.mult))
                settle()
                pool.tensor_tensor(mix[:, j, 1, :], wts[:, w, :], mix[:, j, 0, :], ALU.subtract).then_inc(S["mix_ready"], 1)

            for j in range(NC):
                rsqrt(j)
                if j == 0:
                    pool.wait_ge(S["vec_in"], 16)
                    pool.wait_ge(S["wts_in"], 16)
                if j < 3:
                    mix_weight(j, (0, 1, 2)[j], (2, 3, 4)[j])
            mix_weight(3, 4, 5)
            mix_weight(4, 5, 6)
            pool.wait_ge(S["slots_ready"], 1)
            pool.wait_ge(S["routed_padded"], 16)
            for t in range(NT):
                pool.indirect_dma_start(routed, bass.IndirectOffsetOnAxis(ap=slot[:, t:t + 1], axis=0),
                                        xn[:, t, :], None, bounds_check=ROWS - 1, oob_is_err=False).then_inc(S["scattered"], 16)
            pool.wait_ge(S["ids_in"], 16)
            for i in range(MT):
                pool.wait_ge(S["moe_y_ready"], i + 1)
                pool.indirect_dma_start(moe, bass.IndirectOffsetOnAxis(ap=row_id[:, i:i + 1], axis=0),
                                        ye[:, i % RING, :], None, bounds_check=T - 1, oob_is_err=False).then_inc(moe_out[i % RING], 16)
            pool.wait_ge(S["moe_y_mm"], MT)
            step(pool.memset(qs32[:, 0:QZ], 0.0))
            settle()
            pool.sem_inc(S["q_zeroed"], 1)
            step(pool.memset(v_aug[:, :, :, HD:HD + 1], 1.0))
            settle()
            pool.sem_inc(S["v_ones"], 1)
            for j in range(NC, 2 * NC):
                rsqrt(j)
            for j in range(NC):
                for s in range(2):
                    pool.wait_ge(S["middle_ready"], 2 * j + s + 1)
                    p = piece[:, j % 2, s]
                    pool.tensor_tensor(p[:, 2, :], left[:, s, :], p[:, 1, :], ALU.subtract).then_inc(S["piece_ready"], 1)
            for j in range(NC):
                pool.wait_ge(S["relu_ready"], j + 1)
                c = slice(CH * j, CH * (j + 1))
                pool.tensor_tensor(buf_a[:, c], buf_a[:, c], buf_a[:, c], ALU.mult).then_inc(S["kact_ready"], 1)

        @block.scalar
        def _(act):
            act.wait_ge(S["vec_in"], 16)
            act.activation(decay[:, :], vec[:, 0:1], ACT.Exp).then_inc(S["decay_exp"], 1)
            for j in range(NC):
                act.wait_ge(S["xT_mm"], j + 1)
                act.activation(xnT[:, 1 + CH * j:1 + CH * (j + 1)], bank[j % 2], ACT.Copy).then_inc(S["xT_ready"], 1)
            for j in range(NC):
                c = slice(CH * j, CH * (j + 1))
                act.wait_ge(S["k_mm"], j + 1)
                act.activation(kf[:, c], bank[2], ACT.Copy).then_inc(S["k_ready"], 1)
                act.wait_ge(S["v_mm"], j + 1)
                act.activation(vf[:, c], bank[3], ACT.Copy).then_inc(S["v_ready"], 1)
                act.wait_ge(S["r_mm"], j + 1)
                act.activation(ef[:, c], bank[4], ACT.Exp, scale=-1.0).then_inc(S["e_ready"], 1)
                if j >= 1:
                    act.wait_ge(S["wkv_args"], j)
                    act.activation(arg[:, j - 1, :, :], arg[:, j - 1, :, :], ACT.Exp).then_inc(S["wkv_exps"], 1)
            act.wait_ge(S["wkv_args"], NC)
            act.activation(arg[:, NC - 1, :, :], arg[:, NC - 1, :, :], ACT.Exp).then_inc(S["wkv_exps"], 1)

            def copy_xT(i, s):
                act.wait_ge(S["moe_xT_mm"], i + 1)
                act.activation(xrT[:, s, :], bank[0][:, 0:P], ACT.Copy).then_inc(S["moe_xT_ready"], 1)

            def gelu(i, s):
                e = act.value_load(te[0:1, bass.ds(i, 1)], min_val=0, max_val=E - 1)
                act.wait_ge(S["moe_h_mm"], i + 1)
                for f in range(NF):
                    g = act.activation(hT[:, s, f * P:(f + 1) * P], bank[5 + s][:, f * P:(f + 1) * P], ACT.Gelu,
                                       bias=b1[:, bass.ds(e * NF + f, 1)])
                g.then_inc(S["moe_h_ready"], 1)

            def copy_y(i, s, before):
                act.wait_ge(S["moe_y_mm"], i + 1)
                if before is not None:
                    act.wait_ge(moe_out[s], before * 16)
                act.activation(ye[:, s, :], bank[1][:, 0:C], ACT.Copy).then_inc(S["moe_y_ready"], 1)

            act.wait_ge(S["experts_in"], 48)
            act.wait_ge(S["slots_ready"], 1)
            copy_xT(0, 0)
            gelu(0, 0)
            copy_xT(1, 1)
            for i in range(RING):
                gelu(i + 1, (i + 1) % RING)
                copy_xT(i + 2, (i + 2) % RING)
                copy_y(i, i, None)
            with act.Fori(1, MT // RING - 1) as r:
                for u in range(RING):
                    i = r * RING + u
                    gelu(i + 1, (u + 1) % RING)
                    copy_xT(i + 2, (u + 2) % RING)
                    copy_y(i, u, r)
            for i in range(MT - RING, MT):
                if i + 1 < MT:
                    gelu(i + 1, (i + 1) % RING)
                if i + 2 < MT:
                    copy_xT(i + 2, (i + 2) % RING)
                copy_y(i, i % RING, i // RING)

            def mixing(j, part):
                c = slice(CH * j, CH * (j + 1))
                if part == 0:
                    act.wait_ge(S["fk_mm"], j + 1)
                    act.activation(buf_a[:, c], bank[0], ACT.Relu).then_inc(S["relu_ready"], 1)
                    act.wait_ge(S["fr_mm"], j + 1)
                    act.activation(buf_b[:, c], bank[1], ACT.Exp, scale=-1.0).then_inc(S["fe_ready"], 1)
                else:
                    act.wait_ge(S["fkv_mm"], j + 1)
                    act.activation(buf_a[:, c], bank[4], ACT.Copy).then_inc(S["fkv_ready"], 1)

            def copy_norm(j):
                act.wait_ge(S["norm_mm"], 2 * j + 1)
                act.activation(norm[:, CH * j:CH * (j + 1)], bank[5][0:H, :], ACT.Copy).then_inc(S["norm_ready"], 1)

            for j in range(NC):
                act.wait_ge(S["xT_mm"], NC + j + 1)
                act.activation(xnT[:, 1 + CH * j:1 + CH * (j + 1)], bank[j % 2], ACT.Copy).then_inc(S["xT_ready"], 1)
                q, k = bank[(2, 6)[j % 2]], bank[(3, 7)[j % 2]]
                if j >= 2:
                    act.wait_ge(q_mid[j - 2], 48)
                    act.wait_ge(k_mid[j - 2], 48)
                    act.wait_ge(S["norm_mm"], 2 * (j - 1))
                act.wait_ge(S["q_mm"], j + 1)
                act.activation(piece[:, j % 2, 0, 0, :], q, ACT.Copy).then_inc(S["q_split"], 1)
                act.activation(sq[:, j % 2, 0, :], q, ACT.Square).then_inc(S["sq_ready"], 1)
                act.wait_ge(S["k2_mm"], j + 1)
                act.activation(piece[:, j % 2, 1, 0, :], k, ACT.Copy).then_inc(S["q_split"], 1)
                act.activation(sq[:, j % 2, 1, :], k, ACT.Square).then_inc(S["sq_ready"], 1)
                act.wait_ge(S["v2_mm"], j + 1)
                if j == 0:
                    act.wait_ge(S["v_ones"], 1)
                act.activation(v_aug[:, TPC * j:TPC * (j + 1), :, 0:HD],
                               bank[4].rearrange("p (t h d) -> p t h d", t=TPC, h=H), ACT.Copy).then_inc(S["v_aug_ready"], 1)
                if j:
                    copy_norm(j - 1)
            copy_norm(NC - 1)
            for j in range(NC):
                mixing(j, 0)
                if j:
                    mixing(j - 1, 1)
            mixing(NC - 1, 1)
            def exps(r):
                for u in range(G * NKT):
                    for half in range(2):
                        n = 2 * u + half
                        act.wait_ge(S["scores_mm"], r * (2 * G * NKT) + n + 1)
                        if u >= 4 and half == 0:
                            act.wait_ge(S["pv_mm"], r * (G * NKT) + u - 3)
                        b = 2 * (n % 3)
                        act.activation(probs[:, u % 4, 2 * half:2 * half + 2, :], psum[:, b:b + 2, :], ACT.Exp, scale=SCALE).then_inc(S["exps_done"], 1)

            with act.Fori(0, NQ) as r:
                exps(r)

        @block.vector
        def _(dve):
            n = [0]

            def step(ins):
                n[0] += 1
                ins.then_inc(S["dve_step"], 1)

            def settle():
                dve.wait_ge(S["dve_step"], n[0])

            def tile_stats(j):
                for t in range(TPC * j, TPC * j + TPC):
                    step(dve.bn_stats(stats[:, t, :], xs[:, t, :]))
                settle()
                for t in range(TPC * j, TPC * j + TPC):
                    step(dve.bn_aggr(mv[:, t, :], stats[:, t, :]))
                settle()
                g = slice(TPC * j, TPC * j + TPC)
                dve.tensor_scalar(veps[:, g], mv[:, g, 1], EPS, None, ALU.add).then_inc(S["ln_var"], 1)

            def normalise(j, turn):
                dve.wait_ge(S["ln_rstd"], turn * NC + j + 1)
                for t in range(TPC * j, TPC * j + TPC):
                    last = dve.tensor_scalar(xn[:, t, 0:C], xs[:, t, :], mv[:, t, 0:1], rstd[:, t:t + 1], ALU.subtract, ALU.mult)
                last.then_inc(S["xn_ready"], 1)

            step(dve.memset(xnT[:, 0:1], 0.0))
            step(dve.memset(m_run[:, 0:1], NEG))
            step(dve.memset(a_run[:, 0:1], 0.0))
            step(dve.memset(b_run[:, 0:1], 0.0))
            for j in range(NC):
                dve.wait_ge(x_in[j], 16)
                tile_stats(j)
                if j:
                    normalise(j - 1, 0)
            normalise(NC - 1, 0)
            dve.wait_ge(S["decay_exp"], 1)
            step(dve.tensor_scalar(decay[:, :], decay[:, :], -1.0, None, ALU.mult))

            dve.wait_ge(S["router_mm"], 1)
            dve.wait_ge(S["const_in"], 32)
            step(dve.tensor_tensor(score[:, :, :], bank[5][:, 0:NT * E].rearrange("p (t e) -> p t e", e=E),
                                   rb[:, :].unsqueeze(1).to_broadcast([P, NT, E]), ALU.add))
            settle()
            step(dve.tensor_reduce(best[:, :], score[:, :, :], AX.X, ALU.max))
            settle()
            step(dve.tensor_tensor(hot[:, :, :], score[:, :, :], best[:, :].unsqueeze(2).to_broadcast([P, NT, E]), ALU.is_equal))
            settle()
            dve.wait_ge(S["ident_ready"], 1)
            step(dve.tensor_tensor(score[:, :, :], hot[:, :, :], rev[:, :].unsqueeze(1).to_broadcast([P, NT, E]), ALU.mult))
            settle()
            step(dve.tensor_reduce(best[:, :], score[:, :, :], AX.X, ALU.max))
            settle()
            dve.tensor_tensor(hot[:, :, :], rev[:, :].unsqueeze(1).to_broadcast([P, NT, E]),
                              best[:, :].unsqueeze(2).to_broadcast([P, NT, E]), ALU.is_equal).then_inc(S["hot_ready"], 1)
            dve.wait_ge(S["prefix_mm"], 1)
            step(dve.tensor_copy(tot[:, :, :], bank[7][:, 0:NT * E].rearrange("p (t e) -> p e t", e=E)))
            settle()
            flat = "p e t -> p (e t)"
            step(dve.tensor_tensor_scan(cum[:, :, :].rearrange(flat), tot[:, :, :].rearrange(flat), tot[:, :, :].rearrange(flat),
                                        0.0, ALU.add, ALU.max))
            step(dve.tensor_reduce(cnt[:, :], tot[:, :, :], AX.X, ALU.add))
            settle()
            step(dve.tensor_tensor(over[:, :, :], cnt[:, :].unsqueeze(2).to_broadcast([P, E, NT]),
                                   full[:, :].unsqueeze(1).to_broadcast([P, E, NT]), ALU.is_gt))
            step(dve.tensor_tensor(adj[:, :], cnt[:, :], cum[:, :, NT - 1], ALU.subtract))
            settle()
            step(dve.tensor_tensor(cum[:, :, :], cum[:, :, :], tot[:, :, :], ALU.subtract))
            step(dve.tensor_reduce(ntile[:, :], over[:, :, :], AX.X, ALU.add))
            settle()
            step(dve.tensor_tensor_scan(tend[:, :], ntile[:, :], ntile[:, :], 0.0, ALU.add, ALU.max))
            settle()
            step(dve.tensor_tensor(ntile[:, :], tend[:, :], ntile[:, :], ALU.subtract))
            step(dve.tensor_tensor(tge[:, :, :], tidx[:, :].unsqueeze(2).to_broadcast([1, MT, E]),
                                   tend[0:1, :].unsqueeze(1).to_broadcast([1, MT, E]), ALU.is_ge))
            settle()
            step(dve.scalar_tensor_tensor(adj[:, :], ntile[:, :], float(P), adj[:, :], ALU.mult, ALU.add))
            step(dve.tensor_reduce(tef[:, :], tge[:, :, :], AX.X, ALU.add))
            settle()
            step(dve.tensor_tensor(cum[:, :, :], cum[:, :, :], adj[:, :].unsqueeze(2).to_broadcast([P, E, NT]), ALU.add))
            step(dve.tensor_scalar(te[:, :], tef[:, :], float(E - 1), None, ALU.min))
            settle()
            step(dve.tensor_tensor(score[:, :, :], bank[6][:, 0:NT * E].rearrange("p (t e) -> p t e", e=E),
                                   cum[:, :, :].rearrange("p e t -> p t e"), ALU.add))
            settle()
            step(dve.tensor_tensor(score[:, :, :], score[:, :, :], hot[:, :, :], ALU.mult))
            settle()
            step(dve.tensor_reduce(slotf[:, :], score[:, :, :], AX.X, ALU.add))
            settle()
            dve.tensor_copy(slot[:, :], slotf[:, :]).then_inc(S["slots_ready"], 1)

            for j in range(NC):
                c, prev = slice(CH * j, CH * (j + 1)), slice(CH * j + 1, CH * (j + 1) + 1)
                dve.wait_ge(S["k_ready"], j + 1)
                settle()
                step(dve.tensor_tensor_scan(m_run[:, prev], decay[:, 0:1].to_broadcast([P, CH]), kf[:, c],
                                            m_run[:, CH * j:CH * j + 1], ALU.add, ALU.max))
                settle()
                step(dve.scalar_tensor_tensor(dd[:, c], kf[:, c], vec[:, 1:2], m_run[:, c], ALU.add, ALU.subtract))
                step(dve.scalar_tensor_tensor(arg[:, j, 0, :], m_run[:, c], decay[:, 0:1], m_run[:, prev], ALU.add, ALU.subtract))
                step(dve.tensor_tensor(arg[:, j, 1, :], kf[:, c], m_run[:, prev], ALU.subtract))
                settle()
                step(dve.tensor_scalar(arg[:, j, 2, :], dd[:, c], -1.0, 0.0, ALU.mult, ALU.min))
                dve.tensor_scalar(arg[:, j, 3, :], dd[:, c], 0.0, None, ALU.min).then_inc(S["wkv_args"], 1)
            for j in range(NC):
                c, prev = slice(CH * j, CH * (j + 1)), slice(CH * j + 1, CH * (j + 1) + 1)
                dve.wait_ge(S["wkv_exps"], j + 1)
                dve.wait_ge(S["v_ready"], j + 1)
                settle()
                step(dve.tensor_tensor(tmp, arg[:, j, 1, :], vf[:, c], ALU.mult))
                step(dve.tensor_tensor_scan(b_run[:, prev], arg[:, j, 0, :], arg[:, j, 1, :], b_run[:, CH * j:CH * j + 1], ALU.mult, ALU.add))
                settle()
                step(dve.tensor_tensor_scan(a_run[:, prev], arg[:, j, 0, :], tmp, a_run[:, CH * j:CH * j + 1], ALU.mult, ALU.add))
                settle()
                step(dve.tensor_tensor(tmp2, arg[:, j, 2, :], a_run[:, c], ALU.mult))
                step(dve.tensor_tensor(arg[:, j, 0, :], arg[:, j, 2, :], b_run[:, c], ALU.mult))
                step(dve.tensor_tensor(arg[:, j, 1, :], arg[:, j, 3, :], vf[:, c], ALU.mult))
                dve.wait_ge(S["e_ready"], j + 1)
                settle()
                step(dve.tensor_tensor(arg[:, j, 0, :], arg[:, j, 0, :], arg[:, j, 3, :], ALU.add))
                settle()
                step(dve.scalar_tensor_tensor(arg[:, j, 0, :], ef[:, c], 1.0, arg[:, j, 0, :], ALU.add, ALU.mult))
                step(dve.tensor_tensor(tmp2, tmp2, arg[:, j, 1, :], ALU.add))
                settle()
                step(dve.reciprocal(arg[:, j, 0, :], arg[:, j, 0, :]))
                settle()
                dve.tensor_tensor(buf_a[:, c], tmp2, arg[:, j, 0, :], ALU.mult).then_inc(S["rwkv_ready"], 1)
            dve.wait_ge(S["rwkv_ready"], NC)
            step(dve.memset(ks32, 0.0))
            settle()
            step(dve.memset(k_stack[0:2, 0, :], 1.0))
            step(dve.memset(k_stack[64:66, 1, :], 1.0))
            settle()
            dve.sem_inc(S["k_zeroed"], 1)
            for j in range(NC):
                xj = xs[:, TPC * j:TPC * (j + 1), :].rearrange("p n c -> p (n c)")
                dve.wait_ge(S["attn_mm"], j + 1)
                step(dve.tensor_tensor(xj, xj, bank[4 + j], ALU.add))
            dve.wait_ge(S["moe_y_mm"], MT)
            step(dve.memset(qs32[:, QZ:], 0.0))
            settle()
            dve.sem_inc(S["q_zeroed"], 1)
            dve.wait_ge(S["moe_in"], 16)
            for j in range(NC):
                xj = xs[:, TPC * j:TPC * (j + 1), :].rearrange("p n c -> p (n c)")
                settle()
                step(dve.tensor_tensor(xj, xj, buf_b[:, CH * j:CH * (j + 1)], ALU.add))
                settle()
                dve.sem_inc(S["x1_ready"], 1)
                tile_stats(j)
                if j:
                    normalise(j - 1, 1)
            normalise(NC - 1, 1)
            def norm_max(j):
                dve.wait_ge(S["norm_ready"], j + 1)
                step(dve.tensor_reduce(nmax[:, 0, j:j + 1], norm[:, CH * j:CH * (j + 1)], AX.X, ALU.max))
                dve.wait_ge(S["norm_mm"], 2 * j + 2)
                dve.tensor_reduce(nmax[:, 1, j:j + 1], bank[5][0:H, :], AX.X, ALU.max).then_inc(S["norms_read"], 1)

            for j in range(NC):
                if j >= 2:
                    dve.wait_ge(q_mid[j - 2], 48)
                    dve.wait_ge(k_mid[j - 2], 48)
                for s in range(2):
                    p = piece[:, j % 2, s]
                    dve.wait_ge(S["sq_ready"], 2 * j + s + 1)
                    if j:
                        dve.wait_ge(S["piece_ready"], 2 * j + s - 1)
                    step(dve.tensor_tensor(left[:, s, :], bank[((2, 6), (3, 7))[s][j % 2]], p[:, 0, :], ALU.subtract))
                    settle()
                    dve.tensor_copy(p[:, 1, :], left[:, s, :]).then_inc(S["middle_ready"], 1)
                if j:
                    norm_max(j - 1)
            norm_max(NC - 1)
            dve.wait_ge(S["norms_read"], NC)
            settle()
            step(dve.tensor_reduce(nbest[:, 0:2], nmax[:, :, :], AX.X, ALU.max))
            settle()
            dve.tensor_tensor(nbest[:, 2:3], nbest[:, 0:1], nbest[:, 1:2], ALU.add).then_inc(S["stack_set"], 1)
            step(dve.tensor_scalar(norm, norm, nbest[:, 1:2], -0.5, ALU.add, ALU.mult))
            dve.wait_ge(S["flag_mm"], 1)
            step(dve.tensor_reduce(flagf[:, :], bank[6][0:1, 0:H], AX.X, ALU.max))
            settle()
            dve.tensor_scalar(flag[:, :], flagf[:, :], SAFE, None, ALU.is_gt).then_inc(S["flag_ready"], 1)
            dve.wait_ge(S["flag_ready"], 1)
            wide = dve.value_load(flag[0:1, 0:1], min_val=0, max_val=1)
            with dve.If(wide):
                dve.sem_inc(S["gmax_read"], 1)
                with dve.Fori(0, H // 2) as g:
                    for half in range(2):
                        with dve.Fori(0, NT) as t:
                            dve.wait_ge(S["gmax_mm"], g * (2 * NT) + half * NT + t + 1)
                            dve.tensor_reduce(top[:, bass.ds(t, 1), bass.ds(g * 2 + half, 1)].rearrange("p a b -> p (a b)"),
                                              psum[:, 0:NC, :], AX.XY, ALU.max).then_inc(S["gmax_read"], 1)
                dve.wait_ge(S["gmax_turned"], 1)
                dve.tensor_scalar(norm, psum[0:H, 0:NC, :].rearrange("h a b -> h (a b)"), -1.0, None, ALU.mult).then_inc(S["gmax_read"], 1)
                dve.wait_ge(S["gmax_read"], H * NT + 2)
            settle()
            step(dve.tensor_copy(shiftp[:, 0, :], norm))
            settle()
            step(dve.tensor_tensor(shiftp[:, 1, :], norm, shiftp[:, 0, :], ALU.subtract))
            settle()
            dve.sem_inc(S["shift_ready"], 1)
            dve.memset(psum[:, 6:8, :], 0.0).then_inc(S["acc_zeroed"], 1)
            dve.sem_inc(S["acc_free"], 2)
            for j in range(NC):
                c = slice(CH * j, CH * (j + 1))
                dve.wait_ge(S["fe_ready"], j + 1)
                step(dve.tensor_scalar(buf_b[:, c], buf_b[:, c], 1.0, None, ALU.add))
                settle()
                step(dve.reciprocal(buf_b[:, c], buf_b[:, c]))
                dve.wait_ge(S["fkv_ready"], j + 1)
                settle()
                dve.tensor_tensor(buf_b[:, c], buf_b[:, c], buf_a[:, c], ALU.mult).then_inc(S["z_ready"], 1)
            base = n[0]
            def divide(r, g):
                dve.wait_ge(S["pv_mm"], r * (G * NKT) + NKT * (g + 1))
                dve.wait_ge(y_packed[g % 2], r * (16 * HG * 2) + 16 * HG * (g // 2) + 16)
                dve.tensor_copy(y_g[:, g % 2, :], bank[6 + g % 2]).then_inc(S["acc_free"], 1)
                dve.wait_ge(S["acc_free"], r * G + g + 3)
                k = r * (3 * G) + (base + 3 * g)
                dve.wait_ge(S["dve_step"], k)
                dve.sem_inc(S["shuffle_turn"], 1)
                dve.stream_shuffle(y_den[:, :], y_g[:, g % 2, :], [HD] * 32).then_inc(S["dve_step"], 1)
                dve.wait_ge(S["dve_step"], k + 1)
                dve.reciprocal(y_den[:, :], y_den[:, :]).then_inc(S["dve_step"], 1)
                dve.wait_ge(S["dve_step"], k + 2)
                dve.tensor_tensor(y_g[:, g % 2, :], y_g[:, g % 2, :], y_den[:, :], ALU.mult).then_inc(S["dve_step"], 1)
                dve.wait_ge(S["dve_step"], k + 3)
                dve.sem_inc(S["y_ready"], 1)

            def finish(j, b):
                xj = xs[:, TPC * j:TPC * (j + 1), :].rearrange("p n c -> p (n c)")
                dve.wait_ge(S["proj_mm"], j + 1)
                dve.tensor_tensor(xj, xj, bank[b], ALU.add).then_inc(S["x1_ready"], 1)

            with dve.Fori(0, NQ - 1) as r:
                for g in range(G):
                    divide(r, g)
            divide(NQ - 1, 0)
            divide(NQ - 1, 1)
            finish(0, 7)
            finish(1, 7)
            divide(NQ - 1, 2)
            finish(2, 6)
            divide(NQ - 1, 3)
            finish(3, 0)

        @block.tensor
        def _(pe):
            pe.wait_ge(S["ident_ready"], 1)

            def transposes(j, turn):
                pe.wait_ge(S["xn_ready"], turn * NC + j + 1)
                if j >= 2:
                    pe.wait_ge(S["xT_ready"], turn * NC + j - 1)
                for t in range(TPC):
                    mm = pe.transpose(bank[j % 2][:, P * t:P * (t + 1)], xn[:, TPC * j + t, 0:C], ident[:, :])
                mm.then_inc(S["xT_mm"], 1)

            def router(j):
                pe.wait_ge(S["xT_ready"], j + 1)
                for t in range(TPC * j, TPC * (j + 1)):
                    mm = pe.matmul(bank[5][:, E * t:E * (t + 1)], xnT[:, 1 + P * t:1 + P * (t + 1)], rw[:, :], start=True, stop=True)
                return mm

            for j in range(NC):
                transposes(j, 0)
                if j == 0:
                    pe.wait_ge(S["const_in"], 32)
                    pe.wait_ge(S["dve_step"], 1)
                mm = router(j)
            mm.then_inc(S["router_mm"], 1)

            def mixed(b, w, j, done, freed):
                if j:
                    pe.wait_ge(freed, j)
                pe.matmul(bank[b], mix[:, w, 0, :], xnT[:, 1 + CH * j:1 + CH * (j + 1)], start=True, stop=False)
                pe.matmul(bank[b], mix[:, w, 1, :], xnT[:, CH * j:CH * (j + 1)], start=False, stop=True).then_inc(done, 1)

            pe.wait_ge(S["mix_ready"], 3)
            for j in range(NC):
                mixed(2, 0, j, S["k_mm"], S["k_ready"])
                if j == 0:
                    pe.wait_ge(S["hot_ready"], 1)
                    hot_f = hot[:, :, :].rearrange("p t e -> p (t e)")
                    pe.matmul(bank[6][:, 0:NT * E], before[:, :], hot_f, start=True, stop=True)
                    pe.matmul(bank[7][:, 0:NT * E], ones[:, :], hot_f, start=True, stop=True).then_inc(S["prefix_mm"], 1)
                mixed(3, 1, j, S["v_mm"], S["v_ready"])
                mixed(4, 2, j, S["r_mm"], S["e_ready"])

            def turn_x(i, s, fills, free=True):
                pe.wait_ge(rows_in[s], 16 * fills)
                if free:
                    pe.wait_ge(S["moe_xT_ready"], i)
                pe.transpose(bank[0][:, 0:P], xr[:, s, :], ident[:, :]).then_inc(S["moe_xT_mm"], 1)

            def up(i, s, fills):
                pe.wait_ge(w1_in[s], 16 * fills)
                pe.wait_ge(S["moe_xT_ready"], i + 1)
                for f in range(NF):
                    mm = pe.matmul(bank[5 + s][:, P * f:P * (f + 1)], w1[:, s, P * f:P * (f + 1)], xrT[:, s, :], start=True, stop=True)
                mm.then_inc(S["moe_h_mm"], 1)

            def down(i, s, free=True):
                e = pe.value_load(te[0:1, bass.ds(i, 1)], min_val=0, max_val=E - 1)
                if free:
                    pe.wait_ge(S["moe_y_ready"], i)
                pe.wait_ge(S["moe_h_ready"], i + 1)
                for f in range(NF):
                    pe.matmul(bank[1][:, 0:C], hT[:, s, P * f:P * (f + 1)], w2[:, bass.ds(e * F + C * f, C)], start=(f == 0), stop=False)
                pe.matmul(bank[1][:, 0:C], ones[0:1, :], b2[0:1, bass.ds(e * C, C)], start=False, stop=True).then_inc(S["moe_y_mm"], 1)

            pe.wait_ge(S["slots_ready"], 1)
            pe.wait_ge(S["experts_in"], 48)
            turn_x(0, 0, 1, False)
            up(0, 0, 1)
            turn_x(1, 1, 1)
            for i in range(RING):
                up(i + 1, (i + 1) % RING, (i + 1) // RING + 1)
                turn_x(i + 2, (i + 2) % RING, (i + 2) // RING + 1)
                down(i, i, i > 0)
            with pe.Fori(1, MT // RING - 1) as r:
                for u in range(RING):
                    i = r * RING + u
                    up(i + 1, (u + 1) % RING, r + (u + 1) // RING + 1)
                    turn_x(i + 2, (u + 2) % RING, r + (u + 2) // RING + 1)
                    down(i, u)
            for i in range(MT - RING, MT):
                if i + 1 < MT:
                    up(i + 1, (i + 1) % RING, (i + 1) // RING + 1)
                if i + 2 < MT:
                    turn_x(i + 2, (i + 2) % RING, (i + 2) // RING + 1)
                down(i, i % RING)
            for j in range(NC):
                pe.wait_ge(S["rwkv_ready"], j + 1)
                for t in range(TPC):
                    k = TPC * j + t
                    mm = pe.matmul(bank[4 + j][:, P * t:P * (t + 1)], buf_a[:, P * k:P * (k + 1)], wts[:, 3, :], start=True, stop=True)
                mm.then_inc(S["attn_mm"], 1)


            pe.wait_ge(S["wq_in"], 32)

            def norms(j):
                for s in range(2):
                    pe.wait_ge(S["sq_ready"], 2 * j + s + 1)
                    if s:
                        pe.wait_ge(S["norm_ready"], j + 1)
                    elif j:
                        pe.wait_ge(S["norms_read"], j)
                    pe.matmul(bank[5][0:H, :], headsel[:, :], sq[:, j % 2, s, :], start=True, stop=True).then_inc(S["norm_mm"], 1)

            for j in range(NC):
                transposes(j, 1)
                pe.wait_ge(S["xT_ready"], NC + j + 1)
                c = slice(1 + CH * j, 1 + CH * (j + 1))
                if j >= 2:
                    pe.wait_ge(S["middle_ready"], 2 * (j - 1))
                pe.matmul(bank[(2, 6)[j % 2]], wqkv[:, 0:C], xnT[:, c], start=True, stop=True).then_inc(S["q_mm"], 1)
                pe.matmul(bank[(3, 7)[j % 2]], wqkv[:, C:2 * C], xnT[:, c], start=True, stop=True).then_inc(S["k2_mm"], 1)
                if j:
                    pe.wait_ge(S["v_aug_ready"], j)
                for t in range(TPC):
                    k = TPC * j + t
                    mm = pe.matmul(bank[4][:, P * t:P * (t + 1)], xnT[:, 1 + P * k:1 + P * (k + 1)], wqkv[:, 2 * C:3 * C], start=True, stop=True)
                mm.then_inc(S["v2_mm"], 1)
                if j:
                    norms(j - 1)
            norms(NC - 1)
            pe.wait_ge(S["v_aug_ready"], NC)

            def mixing_v(j):
                pe.wait_ge(S["kact_ready"], j + 1)
                if j:
                    pe.wait_ge(S["fkv_ready"], j)
                pe.matmul(bank[4], wts[:, 6, :], buf_a[:, CH * j:CH * (j + 1)], start=True, stop=True).then_inc(S["fkv_mm"], 1)

            for j in range(NC):
                for w, b, done, freed in ((4, 0, "fk_mm", "relu_ready"), (3, 1, "fr_mm", "fe_ready")):
                    if j:
                        pe.wait_ge(S[freed], j)
                    pe.matmul(bank[b], mix[:, w, 0, :], xnT[:, 1 + CH * j:1 + CH * (j + 1)], start=True, stop=False)
                    pe.matmul(bank[b], mix[:, w, 1, :], xnT[:, CH * j:CH * (j + 1)], start=False, stop=True).then_inc(S[done], 1)
                if j:
                    mixing_v(j - 1)
                    continue
                pe.wait_ge(S["stack_set"], 1)
                pe.transpose(bank[6][0:1, 0:H], nbest[:, 2:3], ident[0:H, 0:H]).then_inc(S["flag_mm"], 1)
            mixing_v(NC - 1)
            pe.wait_ge(S["relu_ready"], NC)
            pe.wait_ge(S["fkv_ready"], NC)
            pe.wait_ge(S["fe_ready"], NC)
            pe.wait_ge(S["flag_ready"], 1)
            wide = pe.value_load(flag[0:1, 0:1], min_val=0, max_val=1)
            with pe.If(wide):
                pe.wait_ge(stack_in, 16 * (2 * NC + 2))
                pe.wait_ge(q_in, 32)
                pe.wait_ge(q_all_in, 32 * (NC - 1))
                with pe.Fori(0, H // 2) as g:
                    for half in range(2):
                        with pe.Fori(0, NT) as t:
                            pe.wait_ge(S["gmax_read"], g * (2 * NT) + half * NT + t + 1)
                            for b in range(NC):
                                mm = pe.matmul(bank[b], q_stack[:, bass.ds(g, 1), bass.ds(t * P, P)].rearrange("p a b -> p (a b)"),
                                               k_stack[:, bass.ds(g * 2 + half, 1), CH * b:CH * (b + 1)].rearrange("p a b -> p (a b)"),
                                               start=True, stop=True)
                            mm.then_inc(S["gmax_mm"], 1)
                pe.wait_ge(S["gmax_read"], H * NT + 1)
                for t in range(NT):
                    mm = pe.transpose(bank[t // TPC][0:H, P * (t % TPC):P * (t % TPC + 1)], top[:, t, :], ident[:, :])
                mm.then_inc(S["gmax_turned"], 1)
                pe.wait_ge(S["gmax_read"], H * NT + 2)
            pe.wait_ge(stack_in, 16 * (2 * NC + 2))
            pe.wait_ge(S["shift_in"], 32)
            pe.wait_ge(S["acc_zeroed"], 1)

            def attend(r, u, project):
                g, kt = divmod(u, NKT)
                pe.wait_ge(S["exps_done"], r * (2 * G * NKT) + 2 * (u + 1))
                if project and u == 3 * NKT:
                    pe.wait_ge(S["x1_ready"], NC + 2)
                if kt == 0:
                    pe.wait_ge(S["acc_free"], r * G + g + 1)
                for h in range(HG):
                    mm = pe.matmul(bank[6 + g % 2][32 * h:32 * h + HD + 1, :], v_aug[:, kt, HG * g + h, :], probs[:, u % 4, h, :],
                                   start=(kt == 0), stop=(kt == NKT - 1))
                mm.then_inc(S["pv_mm"], 1)

            def scores(r, u, wrap):
                g, kt = divmod(u, NKT)
                for half in range(2):
                    n = 2 * u + half
                    if n >= 3:
                        pe.wait_ge(S["exps_done"], r * (2 * G * NKT) + n - 2)
                    elif wrap and n < 2:
                        pe.wait_ge(S["exps_done"], r * (2 * G * NKT) + n - 1)
                    for h in range(2):
                        hh = HG * g + 2 * half + h
                        mm = pe.matmul(bank[2 * (n % 3) + h], k_stack[:, hh, P * kt:P * (kt + 1)],
                                       q_stack[:, hh // 2, bass.ds(r * CH, CH)], start=True, stop=True)
                    mm.then_inc(S["scores_mm"], 1)

            def project(j, b):
                for t in range(TPC):
                    k = TPC * j + t
                    pe.matmul(bank[b][:, P * t:P * (t + 1)], yT[:, P * k:P * (k + 1)], wo1[:, :], start=True, stop=False)
                    mm = pe.matmul(bank[b][:, P * t:P * (t + 1)], buf_b[:, P * k:P * (k + 1)], ident[:, :], start=False, stop=True)
                mm.then_inc(S["proj_mm"], 1)

            def query_block(r, last):
                for u in range(G * NKT):
                    if u + 1 < G * NKT:
                        scores(r, u + 1, False)
                    elif not last:
                        pe.wait_ge(q_in, r * 32 + 64)
                        scores(r + 1, 0, True)
                    attend(r, u, last)
                    if last and u == 2 * NKT + 1:
                        pe.wait_ge(S["acc_free"], r * G + 4)
                        pe.wait_ge(S["z_ready"], NC)
                        project(0, 7)
                    if last and u == 2 * NKT + 8:
                        pe.wait_ge(S["x1_ready"], NC + 1)
                        project(1, 7)
                    if last and u == 3 * NKT + 4:
                        pe.wait_ge(S["acc_free"], r * G + 5)
                        project(2, 6)

            pe.wait_ge(q_in, 32)
            scores(0, 0, False)
            with pe.Fori(0, NQ - 1) as r:
                query_block(r, False)
            query_block(NQ - 1, True)
            for s in range(2):
                pe.wait_ge(y_packed[s], 16 * HG * NQ * 2 + 16)
            pe.wait_ge(S["exps_done"], NQ * 2 * G * NKT)
            project(NQ - 1, 0)


_OUTS = [((1, 2048, 128), "float32")]


def kernel(**inputs):
    import numpy as np
    import concourse.bacc as bacc
    from concourse import mybir as mb
    from concourse.bass_utils import run_bass_kernel_spmd as run

    a = {k: np.asarray(v) for k, v in inputs.items()}
    flat = lambda v: np.reshape(v, (-1,))
    vecs = np.stack([flat(a[k]) for k in ("L0_attn_W", "L0_attn_U", "L0_attn_time_mix_k", "L0_attn_time_mix_v",
                                          "L0_attn_time_mix_r", "L1_ffn_mu_r", "L1_ffn_mu_k")], axis=1)
    w_t = np.concatenate([a[k].T for k in ("L0_attn_Wk", "L0_attn_Wv", "L0_attn_Wr", "L0_attn_Wo",
                                           "L1_ffn_W_r", "L1_ffn_W_k", "L1_ffn_W_v")], axis=1)
    w1, b1, w2 = a["L0_ffn_w1"], a["L0_ffn_b1"], a["L0_ffn_w2"]
    e, f, h = w2.shape
    w2r = np.transpose(np.reshape(w2, (e, f // 128, 128, h)), (0, 2, 1, 3)).reshape(e, 128, f // 128 * h)
    b1r = np.transpose(np.reshape(b1, (e, f // 128, 128)), (0, 2, 1))
    expert_b1 = np.transpose(b1r, (1, 0, 2)).reshape(128, -1)
    arrays = {"in_x": a["L0_attn_x"], "in_vecs": vecs, "in_w_t": w_t, "in_router_w": a["L0_ffn_wr"],
              "in_router_b": a["L0_ffn_br"], "in_expert_w1": w1, "in_expert_w2": w2r, "in_expert_b1": expert_b1,
              "in_expert_b2": np.reshape(a["L0_ffn_b2"], (1, -1)),
              "in_w_qkv": a["L1_attn_w_qkv"], "in_w_out": a["L1_attn_w_out"]}
    arrays = {k: np.ascontiguousarray(v) for k, v in arrays.items()}
    nc = bacc.Bacc("TRN2", target_bir_lowering=False, num_devices=1)
    args = [nc.dram_tensor(k, v.shape, mb.dt.from_np(v.dtype), kind="ExternalInput").ap() for k, v in arrays.items()]
    for i, (shape, dtype) in enumerate(_OUTS):
        args.append(nc.dram_tensor(f"out_{i}", shape, mb.dt.from_np(np.dtype(dtype)), kind="ExternalOutput").ap())
    two_layer_kernel(nc, *args)
    r = run(nc, [arrays], core_ids=[0])
    return r.results[0]["out_0"]
```

```python
import concourse.bass as bass
from concourse import mybir
from contextlib import ExitStack


def two_layer_kernel(nc: bass.Bass, x, vecs, w_t, router_w, router_b, expert_w1, expert_w2, expert_b1, expert_b2, w_qkv, w_out, out):
    fp32, bf16 = mybir.dt.float32, mybir.dt.bfloat16
    i32, u32 = mybir.dt.int32, mybir.dt.uint32
    ALU, ACT, AX = mybir.AluOpType, mybir.ActivationFunctionType, mybir.AxisListType

    P = 128
    T, C = x.shape[1], x.shape[2]
    NT = T // P
    CH = 512
    NC = T // CH
    TPC = CH // P
    E = router_w.shape[1]
    F = expert_w1.shape[2]
    NF = F // P
    RING = 3
    MT = NT + E - 1
    RUN = (MT - 2) // RING
    ROWS = MT * P
    XW = C + 4
    H, HD = 16, 8
    G, HG = 4, 4
    NKT = T // P
    NQ = T // CH
    assert NQ == NC == G == 4
    SCALE = float(HD) ** -0.5
    NEG = -1e38
    EPS = 1e-5
    SAFE = 226.0

    x_t = x.rearrange("a (n p) c -> p (a n) c", p=P)
    out_t = out.rearrange("a (n p) c -> p (a n) c", p=P)
    routed = nc.dram_tensor("routed", (ROWS, XW), fp32, kind="Internal").ap()
    moe = nc.dram_tensor("moe", (T, C), fp32, kind="Internal").ap()
    moe_t = moe.rearrange("(n p) c -> p n c", p=P)
    NB = 6
    stacked = nc.dram_tensor("stacked", (2, C, NB, T), bf16, kind="Internal").ap()
    shifts = nc.dram_tensor("shifts", (H, 2, T), bf16, kind="Internal").ap()
    ROW0 = 8

    ctx = ExitStack()
    with ctx:
        def sb(name, shape, dt=fp32):
            return ctx.enter_context(nc.sbuf_tensor(name, shape, dt))

        def sem(name):
            return ctx.enter_context(nc.semaphore(name))

        psum = ctx.enter_context(nc.psum_tensor("psum", [P, 8, CH], fp32))
        bank = [psum[:, i, :] for i in range(8)]

        xs = sb("xs", [P, NT, C])
        xn = sb("xn", [P, NT, XW])
        xnT = sb("xnT", [P, T + 1])
        buf_a = sb("buf_a", [P, T])
        buf_b = sb("buf_b", [P, T])
        ident = sb("ident", [P, P])
        ones = sb("ones", [P, P])
        before = sb("before", [P, P])
        vec = sb("vec", [P, 7])
        wts = sb("wts", [P, 7, C])
        mix = sb("mix", [P, 5, 2, C])
        wqkv = sb("wqkv", [P, 3 * C])
        wo1 = sb("wo1", [P, C])
        wo_last = sb("wo_last", [P, C])
        stats = sb("stats", [P, NT, 6])
        mv = sb("mv", [P, NT, 2])
        veps = sb("veps", [P, NT])
        halves = sb("halves", [P, NT])
        rstd = sb("rstd", [P, NT])
        pad = sb("pad", [P, XW])

        k_stack = sb("k_stack", [P, H, T], bf16)
        q_stack = sb("q_stack", [P, H // 2, T], bf16)
        probs = sb("probs", [P, 4, HG, CH])
        v_aug = sb("v_aug", [P, NKT, H, HD + 1])
        yT = xn[:, :, :].rearrange("p n c -> p (n c)")[:, 0:T]
        y_work = sb("y_work", [P, 3 * CH])
        y_g = y_work[:, 0:2 * CH].rearrange("p (s t) -> p s t", s=2)
        y_den = y_work[:, 2 * CH:3 * CH]

        QZ = 5632
        ks32 = k_stack[:, :, :].rearrange("p h t -> p (h t)").bitcast(fp32)
        arg = ks32[:, 0:4 * T].rearrange("p (j a t) -> p j a t", j=NC, a=4)
        kf, vf, ef, dd = (ks32[:, (4 + i) * T:(5 + i) * T] for i in range(4))
        pr32 = probs[:, :, :, :].rearrange("p a h t -> p (a h t)")
        m_run, a_run, b_run = (pr32[:, i * (T + 1):(i + 1) * (T + 1)] for i in range(3))
        tmp = pr32[:, 3 * (T + 1):3 * (T + 1) + CH]
        tmp2 = pr32[:, 3 * (T + 1) + CH:3 * (T + 1) + 2 * CH]
        qs32 = q_stack[:, :, :].rearrange("p h t -> p (h t)").bitcast(fp32)
        w2 = qs32[:, 0:E * F]
        w1 = qs32[:, E * F:E * F + RING * F].rearrange("p (s n) -> p s n", s=RING)
        xr = buf_b[:, 0:RING * C].rearrange("p (s n) -> p s n", s=RING)
        ye = buf_b[:, RING * C:2 * RING * C].rearrange("p (s n) -> p s n", s=RING)
        row_id = buf_b[:, 2 * RING * C:2 * RING * C + MT].bitcast(u32)
        va32 = v_aug[:, :, :, :].rearrange("p n h d -> p (n h d)")
        hT = va32[:, 0:RING * F].rearrange("p (s n) -> p s n", s=RING)
        xrT = va32[:, RING * F:RING * (F + P)].rearrange("p (s n) -> p s n", s=RING)
        b1 = sb("b1", [P, E * NF])
        spare = sb("spare", [P, E * C])
        b2 = spare[0:1, :]

        rb = sb("rb", [P, E])
        rw = sb("rw", [P, E])
        score = sb("score", [P, NT, E])
        best = sb("best", [P, NT])
        rev = sb("rev", [P, E])
        hot = sb("hot", [P, NT, E])
        tot = sb("tot", [P, E, NT])
        cum = sb("cum", [P, E, NT])
        cnt = sb("cnt", [P, E])
        full = sb("full", [P, NT])
        over = sb("over", [P, E, NT])
        ntile = sb("ntile", [P, E])
        tend = sb("tend", [P, E])
        adj = sb("adj", [P, E])
        slotf = sb("slotf", [P, NT])
        slot = sb("slot", [P, NT], u32)
        tidx = sb("tidx", [1, MT])
        tge = sb("tge", [1, MT, E])
        tef = sb("tef", [1, MT])
        te = sb("te", [1, MT], i32)
        probe = sb("probe", [P, 1])
        decay = sb("decay", [P, 1])

        at = [0]

        def ppart(words):
            at[0] += words
            return pr32[:, at[0] - words:at[0]]

        PW = 3 * CH // 2
        piece_words = [[ppart(PW), spare[:, 0:PW], y_work[:, 0:PW], y_work[:, PW:2 * PW]], [ppart(PW) for j in range(NC)]]
        piece = [[w.bitcast(bf16).rearrange("p (k t) -> p k t", k=3) for w in of] for of in piece_words]
        left = ppart(2 * CH).rearrange("p (s t) -> p s t", s=2)
        sq = ppart(2 * CH).bitcast(bf16).rearrange("p (r s t) -> p r s t", r=2, s=2)
        top = ppart(NT * H).rearrange("p (n h) -> p n h", n=NT)
        norm = ppart(T)[0:H, :]
        assert at[0] <= pr32.shape[1]
        shiftp = xn[:, :, :].rearrange("p n c -> p (n c)")[0:H, 0:T].bitcast(bf16).rearrange("h (k t) -> h k t", k=2)
        headsel = sb("headsel", [P, H], bf16)
        nmax = sb("nmax", [H, 2, NC])
        nbest = sb("nbest", [H, 3])
        flagf = sb("flagf", [1, 1])
        flag = sb("flag", [1, 1], i32)

        names = """vec_in wts_in wq_in const_in routed_padded pool_step dve_step ident_ready decay_exp mix_ready ln_var ln_rstd xn_ready
            xT_mm xT_ready router_mm hot_ready prefix_mm slots_ready k_mm v_mm r_mm k_ready v_ready e_ready
            wkv_args wkv_exps rwkv_ready scattered moe_xT_mm moe_xT_ready moe_h_mm moe_h_ready
            moe_y_mm moe_y_ready shuffle_turn moe_in experts_in wo_last_in probed pad_ready v_ones ids_in attn_mm x1_ready
            act_step q_mm k2_mm v2_mm q_split norm_mm norms_read flag_mm flag_ready v_aug_ready k_zeroed q_zeroed
            middle_ready norm_ready piece_ready shift_ready shift_mid shift_in sq_ready gmax_mm gmax_read gmax_turned wide_step stack_set
            fk_mm fr_mm fkv_mm relu_ready kact_ready fe_ready fkv_ready z_ready
            scores_mm exps_done pv_mm acc_free acc_zeroed tail_step y_ready proj_mm""".split()
        S = {n: sem(n) for n in names}
        x_in = [sem(f"x_in{j}") for j in range(NC)]
        w1_in = [sem(f"w1_in{s}") for s in range(RING)]
        rows_in = [sem(f"rows_in{s}") for s in range(RING)]
        moe_out = [sem(f"moe_out{s}") for s in range(RING)]
        q_mid = [sem(f"q_mid{j}") for j in range(NC)]
        k_mid = [sem(f"k_mid{j}") for j in range(NC)]
        stack_in, q_in, q_all_mid, q_all_in = sem("stack_in"), sem("q_in"), sem("q_all_mid"), sem("q_all_in")
        y_packed = [sem(f"y_packed{i}") for i in range(2)]
        done_out = sem("done_out")
        block = ctx.enter_context(nc.Block())

        @block.sync
        def _(sp):
            for j in range(NC):
                sp.dma_start(xs[:, TPC * j:TPC * (j + 1), :], x_t[:, TPC * j:TPC * (j + 1), :]).then_inc(x_in[j], 16)
            sp.dma_start(rw[:, :], router_w).then_inc(S["const_in"], 16)
            sp.dma_start(rb[:, :], router_b.partition_broadcast(P)).then_inc(S["const_in"], 16)
            sp.dma_start(vec[:, :], vecs).then_inc(S["vec_in"], 16)
            sp.dma_start(wts[:, :, :], w_t.rearrange("p (m n) -> p m n", m=7)).then_inc(S["wts_in"], 16)
            sp.wait_ge(S["pad_ready"], 1)
            rt = routed.rearrange("(m p) c -> p m c", p=P)
            sp.dma_start(rt, pad[:, :].unsqueeze(1).to_broadcast([P, MT, XW])).then_inc(S["routed_padded"], 16)
            sp.dma_start(w2.rearrange("p (e n) -> p e n", e=E), expert_w2.rearrange("e p n -> p e n")).then_inc(S["experts_in"], 16)
            sp.dma_start(b1[:, :], expert_b1).then_inc(S["experts_in"], 16)
            sp.dma_start(b2, expert_b2).then_inc(S["experts_in"], 16)
            sp.dma_start(wqkv[:, :], w_qkv).then_inc(S["wq_in"], 16)
            sp.dma_start(wo1[:, :], w_out).then_inc(S["wq_in"], 16)
            for h in range(HG):
                sp.dma_start(wo_last[32 * h:32 * h + HD, :], w_out[C - HG * HD + HD * h:C - HG * HD + HD * (h + 1), :]).then_inc(S["wo_last_in"], 16)
            def load_w1(i, s):
                e = sp.value_load(te[0:1, bass.ds(i, 1)], min_val=0, max_val=E - 1)
                sp.dma_start(w1[:, s, :], expert_w1[bass.ds(e, 1), :, :].rearrange("a p n -> p (a n)")).then_inc(w1_in[s], 16)

            sp.wait_ge(S["slots_ready"], 1)
            for s in range(RING):
                load_w1(s, s)
            def load_rows(i, s):
                sp.dma_start(xr[:, s, :], routed[bass.ds(i * P, P), 0:C]).then_inc(rows_in[s], 16)

            sp.wait_ge(S["scattered"], 16 * NT)
            for s in range(RING):
                load_rows(s, s)
            with nc.allow_non_contiguous_dma(reason="one word of each row"):
                sp.dma_start(row_id, rt[:, :, C].bitcast(u32)).then_inc(S["ids_in"], 16)
            def reload(i, s):
                sp.wait_ge(S["moe_h_mm"], i - RING + 1)
                load_rows(i, s)
                load_w1(i, s)

            with sp.Fori(1, MT // RING) as r:
                for s in range(RING):
                    reload(r * RING + s, s)
            for i in range(MT // RING * RING, MT):
                reload(i, i % RING)
            sp.wait_ge(S["k_zeroed"], 1)
            for half in range(2):
                one = k_stack[64 * half:64 * half + 2, half:half + 1, :]
                sp.dma_start(k_stack[64 * half:64 * half + 2, half + 2:H:2, :], one.to_broadcast([2, H // 2 - 1, T])).then_inc(stack_in, 16)
            for s in range(RING):
                sp.wait_ge(moe_out[s], 16 * len(range(s, MT, RING)))
            sp.dma_start(buf_b.rearrange("p (n c) -> p n c", n=NT), moe_t).then_inc(S["moe_in"], 16)
            def load_stack(s, c, done):
                for half in range(2):
                    rows = slice(64 * half + ROW0, 64 * half + ROW0 + NB * HD)
                    src = stacked_rows[s][half][:, :, c]
                    dst = q_stack[rows, :, c] if s == 0 else k_stack[rows, half:H:2, c]
                    sp.dma_start(dst, src).then_inc(done, 16)

            stacked_rows = [[stacked[s].rearrange("(g a d) b t -> a (d b) g t", a=2, d=HD)[half] for half in range(2)] for s in range(2)]

            def store_q(j, done):
                for k, b, m in ((0, 0, 3), (1, 3, 2), (2, 5, 1)):
                    sp.dma_start(stacked[0, :, b:b + m, CH * j:CH * (j + 1)], piece[0][j][:, k:k + 1, :].to_broadcast([P, m, CH])).then_inc(done, 16)

            for j in range(NC):
                c = slice(CH * j, CH * (j + 1))
                sp.wait_ge(S["piece_ready"], 2 * j + 1)
                for b, m in ((0, 3), (3, 2), (5, 1)):
                    sp.dma_start(stacked[1, :, b:b + m, c], piece[1][j][:, 0:m, :]).then_inc(k_mid[j], 16)
                if j == 0:
                    sp.wait_ge(S["piece_ready"], 2)
                    store_q(0, q_mid[0])
                sp.wait_ge(k_mid[j], 48)
                load_stack(1, c, stack_in)
                if j == 0:
                    sp.wait_ge(S["q_zeroed"], 2)
                    sp.wait_ge(q_mid[0], 48)
                    load_stack(0, c, q_in)
            sp.wait_ge(S["flag_ready"], 1)
            wide = sp.value_load(flag[0:1, 0:1], min_val=0, max_val=1)
            with sp.If(wide):
                sp.wait_ge(S["piece_ready"], 2 * NC)
                for j in range(1, NC):
                    store_q(j, q_all_mid)
                sp.wait_ge(q_all_mid, 48 * (NC - 1))
                for j in range(1, NC):
                    load_stack(0, slice(CH * j, CH * (j + 1)), q_all_in)
                sp.wait_ge(q_all_in, 32 * (NC - 1))
            sp.wait_ge(S["shift_ready"], 1)
            sp.dma_start(shifts, shiftp).then_inc(S["shift_mid"], 16)
            sp.wait_ge(S["shift_mid"], 16)
            for half in range(2):
                sp.dma_start(q_stack[64 * half:64 * half + 2, :, :],
                             shifts.rearrange("(g a) k t -> a k g t", a=2)[half]).then_inc(S["shift_in"], 16)
            sp.wait_ge(S["piece_ready"], 2 * NC)
            for j in range(1, NC):
                store_q(j, q_mid[j])
            for s in range(2):
                sp.sem_inc(y_packed[s], 16)
            def pack(r, g):
                sp.wait_ge(S["y_ready"], r * G + g + 1)
                for h in range(HG):
                    sp.dma_start(yT[32 * g + HD * h:32 * g + HD * (h + 1), bass.ds(r * CH, CH)],
                                 y_g[32 * h:32 * h + HD, g % 2, :]).then_inc(y_packed[g % 2], 16)

            def store(j):
                sp.wait_ge(S["x1_ready"], NC + j + 1)
                sp.dma_start(out_t[:, TPC * j:TPC * (j + 1), :], xs[:, TPC * j:TPC * (j + 1), :]).then_inc(done_out, 16)

            for j in range(1, NC):
                sp.wait_ge(q_mid[j], 48)
            with sp.Fori(0, NQ - 1) as r:
                sp.wait_ge(q_in, r * 32 + 32)
                load_stack(0, bass.ds(r * CH + CH, CH), q_in)
                for g in range(G):
                    pack(r, g)
            pack(NQ - 1, 0)
            pack(NQ - 1, 1)
            store(0)
            store(1)
            pack(NQ - 1, 2)
            store(2)
            for half in range(2):
                n = TPC * (NC - 1) + half * TPC // 2
                sp.wait_ge(S["x1_ready"], 2 * NC + half)
                sp.dma_start(out_t[:, n:n + TPC // 2, :], xs[:, n:n + TPC // 2, :]).then_inc(done_out, 16)
            sp.wait_ge(done_out, 16 * (NC + 1))

        @block.gpsimd
        def _(pool):
            n = [0]

            def step(ins):
                n[0] += 1
                ins.then_inc(S["pool_step"], 1)

            def settle():
                pool.wait_ge(S["pool_step"], n[0])

            step(pool.memset(pad[:, :], 0.0))
            step(pool.memset(wo_last[:, :], 0.0))
            settle()
            step(pool.memset(pad[:, C:C + 1].bitcast(i32), T))
            settle()
            pool.sem_inc(S["pad_ready"], 1)
            step(pool.memset(ones[:, :], 1.0))
            step(pool.memset(halves[:, :], -0.5))
            step(pool.iota(xn[:, :, C:C + 1].bitcast(i32), pattern=[[P, NT]], base=0, channel_multiplier=1))
            step(pool.iota(rev[:, :], pattern=[[-1, E]], base=E, channel_multiplier=0, allow_small_or_imprecise_dtypes=True))
            step(pool.iota(full[:, :], pattern=[[P, NT]], base=0, channel_multiplier=0, allow_small_or_imprecise_dtypes=True))
            step(pool.iota(tidx[:, :], pattern=[[1, MT]], base=0, channel_multiplier=0, allow_small_or_imprecise_dtypes=True))
            step(pool.memset(xn[:, :, C + 1:XW], 0.0))
            settle()
            step(pool.affine_select(out=ident[:, :], in_=ones[:, :], compare_op=ALU.is_equal, fill=0.0,
                                    base=0, pattern=[[-1, P]], channel_multiplier=1))
            step(pool.affine_select(out=before[:, :], in_=ones[:, :], compare_op=ALU.is_gt, fill=0.0,
                                    base=0, pattern=[[1, P]], channel_multiplier=-1))
            settle()
            pool.sem_inc(S["ident_ready"], 1)
            step(pool.affine_select(out=headsel[:, :], in_=ones[:, 0:H], compare_op=ALU.is_ge, fill=0.0,
                                    base=0, pattern=[[-HD, H]], channel_multiplier=1))
            settle()
            step(pool.affine_select(out=headsel[:, :], in_=headsel[:, :], compare_op=ALU.is_ge, fill=0.0,
                                    base=HD - 1, pattern=[[HD, H]], channel_multiplier=-1))

            def rsqrt(j):
                pool.wait_ge(S["ln_var"], j + 1)
                g = slice(TPC * (j % NC), TPC * (j % NC) + TPC)
                pool.tensor_tensor(rstd[:, g], veps[:, g], halves[:, g], ALU.pow).then_inc(S["ln_rstd"], 1)

            def mix_weight(j, w, v):
                step(pool.tensor_scalar(mix[:, j, 0, :], wts[:, w, :], vec[:, v:v + 1], None, ALU.mult))
                settle()
                pool.tensor_tensor(mix[:, j, 1, :], wts[:, w, :], mix[:, j, 0, :], ALU.subtract).then_inc(S["mix_ready"], 1)

            for j in range(NC):
                rsqrt(j)
                if j == 0:
                    pool.wait_ge(S["vec_in"], 16)
                    pool.wait_ge(S["wts_in"], 16)
                if j < 3:
                    mix_weight(j, (0, 1, 2)[j], (2, 3, 4)[j])
            mix_weight(3, 4, 5)
            mix_weight(4, 5, 6)
            pool.wait_ge(S["slots_ready"], 1)
            pool.wait_ge(S["routed_padded"], 16)
            for t in range(NT):
                pool.indirect_dma_start(routed, bass.IndirectOffsetOnAxis(ap=slot[:, t:t + 1], axis=0),
                                        xn[:, t, :], None, bounds_check=ROWS - 1, oob_is_err=False).then_inc(S["scattered"], 16)
            pool.wait_ge(S["ids_in"], 16)
            for i in range(MT):
                pool.wait_ge(S["moe_y_ready"], i + 1)
                pool.indirect_dma_start(moe, bass.IndirectOffsetOnAxis(ap=row_id[:, i:i + 1], axis=0),
                                        ye[:, i % RING, :], None, bounds_check=T - 1, oob_is_err=False).then_inc(moe_out[i % RING], 16)
            pool.wait_ge(S["moe_y_mm"], MT)
            step(pool.memset(qs32[:, 0:QZ], 0.0))
            settle()
            pool.sem_inc(S["q_zeroed"], 1)
            step(pool.memset(v_aug[:, :, :, HD:HD + 1], 1.0))
            settle()
            pool.sem_inc(S["v_ones"], 1)
            for j in range(NC, 2 * NC):
                rsqrt(j)
            for j in range(NC + 1):
                if j < NC:
                    for s in (1, 0):
                        pool.wait_ge(S["middle_ready"], 2 * j + 2 - s)
                        p = piece[s][j]
                        pool.tensor_tensor(p[:, 2, :], left[:, s, :], p[:, 1, :], ALU.subtract).then_inc(S["piece_ready"], 1)
                if j:
                    pool.wait_ge(S["relu_ready"], j)
                    c = slice(CH * (j - 1), CH * j)
                    pool.tensor_tensor(buf_a[:, c], buf_a[:, c], buf_a[:, c], ALU.mult).then_inc(S["kact_ready"], 1)

        @block.scalar
        def _(act):
            act.wait_ge(S["vec_in"], 16)
            act.activation(decay[:, :], vec[:, 0:1], ACT.Exp).then_inc(S["decay_exp"], 1)
            for j in range(NC):
                act.wait_ge(S["xT_mm"], j + 1)
                act.activation(xnT[:, 1 + CH * j:1 + CH * (j + 1)], bank[j % 2], ACT.Copy).then_inc(S["xT_ready"], 1)
            for j in range(NC):
                c = slice(CH * j, CH * (j + 1))
                act.wait_ge(S["k_mm"], j + 1)
                act.activation(kf[:, c], bank[2], ACT.Copy).then_inc(S["k_ready"], 1)
                act.wait_ge(S["v_mm"], j + 1)
                act.activation(vf[:, c], bank[3], ACT.Copy).then_inc(S["v_ready"], 1)
                act.wait_ge(S["r_mm"], j + 1)
                act.activation(ef[:, c], bank[4], ACT.Exp, scale=-1.0).then_inc(S["e_ready"], 1)
                if j >= 1:
                    act.wait_ge(S["wkv_args"], j)
                    act.activation(arg[:, j - 1, :, :], arg[:, j - 1, :, :], ACT.Exp).then_inc(S["wkv_exps"], 1)
            act.wait_ge(S["wkv_args"], NC)
            act.activation(arg[:, NC - 1, :, :], arg[:, NC - 1, :, :], ACT.Exp).then_inc(S["wkv_exps"], 1)

            def copy_xT(i, s):
                act.wait_ge(S["moe_xT_mm"], i + 1)
                act.activation(xrT[:, s, :], bank[0][:, 0:P], ACT.Copy).then_inc(S["moe_xT_ready"], 1)

            def gelu(i, s):
                e = act.value_load(te[0:1, bass.ds(i, 1)], min_val=0, max_val=E - 1)
                act.wait_ge(S["moe_h_mm"], i + 1)
                for f in range(NF):
                    g = act.activation(hT[:, s, f * P:(f + 1) * P], bank[5 + s][:, f * P:(f + 1) * P], ACT.Gelu,
                                       bias=b1[:, bass.ds(e * NF + f, 1)])
                g.then_inc(S["moe_h_ready"], 1)

            def copy_y(i, s, before):
                act.wait_ge(S["moe_y_mm"], i + 1)
                if before is not None:
                    act.wait_ge(moe_out[s], before * 16)
                act.activation(ye[:, s, :], bank[1][:, 0:C], ACT.Copy).then_inc(S["moe_y_ready"], 1)

            act.activation(probe[:, :], decay[:, :], ACT.Gelu).then_inc(S["probed"], 1)
            act.wait_ge(S["experts_in"], 48)
            act.wait_ge(S["slots_ready"], 1)
            copy_xT(0, 0)
            copy_xT(1, 1)
            gelu(0, 0)
            for i in range(RING):
                copy_xT(i + 2, (i + 2) % RING)
                gelu(i + 1, (i + 1) % RING)
                copy_y(i, i, None)
            with act.Fori(1, RUN) as r:
                for u in range(RING):
                    i = r * RING + u
                    copy_xT(i + 2, (u + 2) % RING)
                    gelu(i + 1, (u + 1) % RING)
                    copy_y(i, u, r)
            for i in range(RING * RUN, MT):
                if i + 2 < MT:
                    copy_xT(i + 2, (i + 2) % RING)
                if i + 1 < MT:
                    gelu(i + 1, (i + 1) % RING)
                copy_y(i, i % RING, i // RING)

            def relu(j):
                act.wait_ge(S["fk_mm"], j + 1)
                act.activation(buf_a[:, CH * j:CH * (j + 1)], bank[6 + j % 2], ACT.Relu).then_inc(S["relu_ready"], 1)

            def exp_r(j):
                act.wait_ge(S["fr_mm"], j + 1)
                act.activation(buf_b[:, CH * j:CH * (j + 1)], bank[6 + j % 2], ACT.Exp, scale=-1.0).then_inc(S["fe_ready"], 1)

            def mixing_v(j):
                act.wait_ge(S["fkv_mm"], j + 1)
                act.activation(buf_a[:, CH * j:CH * (j + 1)], bank[2 + j % 2], ACT.Copy).then_inc(S["fkv_ready"], 1)

            def copy_norm(j):
                act.wait_ge(S["norm_mm"], 2 * j + 1)
                act.activation(norm[:, CH * j:CH * (j + 1)], bank[5][0:H, :], ACT.Copy).then_inc(S["norm_ready"], 1)

            def copy_turned(j):
                act.wait_ge(S["xT_mm"], NC + j + 1)
                act.activation(xnT[:, 1 + CH * j:1 + CH * (j + 1)], bank[j % 2], ACT.Copy).then_inc(S["xT_ready"], 1)

            copy_turned(0)
            for j in range(NC):
                if j + 1 < NC:
                    copy_turned(j + 1)
                if j >= 2:
                    act.wait_ge(S["norm_mm"], 2 * (j - 1))
                for s, done in ((1, "k2_mm"), (0, "q_mm")):
                    act.wait_ge(S[done], j + 1)
                    act.activation(piece[s][j][:, 0, :], bank[2 + s], ACT.Copy).then_inc(S["q_split"], 1)
                    act.activation(sq[:, j % 2, s, :], bank[2 + s], ACT.Square).then_inc(S["sq_ready"], 1)
                act.wait_ge(S["v2_mm"], j + 1)
                if j == 0:
                    act.wait_ge(S["v_ones"], 1)
                act.activation(v_aug[:, TPC * j:TPC * (j + 1), :, 0:HD],
                               bank[4].rearrange("p (t h d) -> p t h d", t=TPC, h=H), ACT.Copy).then_inc(S["v_aug_ready"], 1)
                if j:
                    copy_norm(j - 1)
                    relu(j - 1)
            copy_norm(NC - 1)
            relu(NC - 1)
            for j in range(NC - 1):
                exp_r(j)
                mixing_v(j)
            mixing_v(NC - 1)
            exp_r(NC - 1)

            def exps(r):
                for u in range(G * NKT):
                    for half in range(2):
                        n = 2 * u + half
                        act.wait_ge(S["scores_mm"], r * (2 * G * NKT) + n + 1)
                        if u >= 4 and half == 0:
                            act.wait_ge(S["pv_mm"], r * (G * NKT) + u - 3)
                        b = 2 * (n % 3)
                        act.activation(probs[:, u % 4, 2 * half:2 * half + 2, :], psum[:, b:b + 2, :], ACT.Exp, scale=SCALE).then_inc(S["exps_done"], 1)

            with act.Fori(0, NQ) as r:
                exps(r)

        @block.vector
        def _(dve):
            n = [0]

            def step(ins):
                n[0] += 1
                ins.then_inc(S["dve_step"], 1)

            def settle():
                dve.wait_ge(S["dve_step"], n[0])

            def tile_stats(j):
                for t in range(TPC * j, TPC * j + TPC):
                    step(dve.bn_stats(stats[:, t, :], xs[:, t, :]))
                settle()
                for t in range(TPC * j, TPC * j + TPC):
                    step(dve.bn_aggr(mv[:, t, :], stats[:, t, :]))
                settle()
                g = slice(TPC * j, TPC * j + TPC)
                dve.tensor_scalar(veps[:, g], mv[:, g, 1], EPS, None, ALU.add).then_inc(S["ln_var"], 1)

            def normalise(j, turn):
                dve.wait_ge(S["ln_rstd"], turn * NC + j + 1)
                for t in range(TPC * j, TPC * j + TPC):
                    last = dve.tensor_scalar(xn[:, t, 0:C], xs[:, t, :], mv[:, t, 0:1], rstd[:, t:t + 1], ALU.subtract, ALU.mult)
                last.then_inc(S["xn_ready"], 1)

            step(dve.memset(xnT[:, 0:1], 0.0))
            step(dve.memset(m_run[:, 0:1], NEG))
            step(dve.memset(a_run[:, 0:1], 0.0))
            step(dve.memset(b_run[:, 0:1], 0.0))
            for j in range(NC):
                dve.wait_ge(x_in[j], 16)
                tile_stats(j)
                if j:
                    normalise(j - 1, 0)
            normalise(NC - 1, 0)
            dve.wait_ge(S["decay_exp"], 1)
            step(dve.tensor_scalar(decay[:, :], decay[:, :], -1.0, None, ALU.mult))

            dve.wait_ge(S["router_mm"], 1)
            dve.wait_ge(S["const_in"], 32)
            step(dve.tensor_tensor(score[:, :, :], bank[5][:, 0:NT * E].rearrange("p (t e) -> p t e", e=E),
                                   rb[:, :].unsqueeze(1).to_broadcast([P, NT, E]), ALU.add))
            settle()
            step(dve.tensor_reduce(best[:, :], score[:, :, :], AX.X, ALU.max))
            settle()
            step(dve.tensor_tensor(hot[:, :, :], score[:, :, :], best[:, :].unsqueeze(2).to_broadcast([P, NT, E]), ALU.is_equal))
            settle()
            dve.wait_ge(S["ident_ready"], 1)
            step(dve.tensor_tensor(score[:, :, :], hot[:, :, :], rev[:, :].unsqueeze(1).to_broadcast([P, NT, E]), ALU.mult))
            settle()
            step(dve.tensor_reduce(best[:, :], score[:, :, :], AX.X, ALU.max))
            settle()
            dve.tensor_tensor(hot[:, :, :], rev[:, :].unsqueeze(1).to_broadcast([P, NT, E]),
                              best[:, :].unsqueeze(2).to_broadcast([P, NT, E]), ALU.is_equal).then_inc(S["hot_ready"], 1)
            dve.wait_ge(S["prefix_mm"], 1)
            step(dve.tensor_copy(tot[:, :, :], bank[7][:, 0:NT * E].rearrange("p (t e) -> p e t", e=E)))
            settle()
            flat = "p e t -> p (e t)"
            step(dve.tensor_tensor_scan(cum[:, :, :].rearrange(flat), tot[:, :, :].rearrange(flat), tot[:, :, :].rearrange(flat),
                                        0.0, ALU.add, ALU.max))
            step(dve.tensor_reduce(cnt[:, :], tot[:, :, :], AX.X, ALU.add))
            settle()
            step(dve.tensor_tensor(over[:, :, :], cnt[:, :].unsqueeze(2).to_broadcast([P, E, NT]),
                                   full[:, :].unsqueeze(1).to_broadcast([P, E, NT]), ALU.is_gt))
            step(dve.tensor_tensor(adj[:, :], cnt[:, :], cum[:, :, NT - 1], ALU.subtract))
            settle()
            step(dve.tensor_tensor(cum[:, :, :], cum[:, :, :], tot[:, :, :], ALU.subtract))
            step(dve.tensor_reduce(ntile[:, :], over[:, :, :], AX.X, ALU.add))
            settle()
            step(dve.tensor_tensor_scan(tend[:, :], ntile[:, :], ntile[:, :], 0.0, ALU.add, ALU.max))
            settle()
            step(dve.tensor_tensor(ntile[:, :], tend[:, :], ntile[:, :], ALU.subtract))
            step(dve.tensor_tensor(tge[:, :, :], tidx[:, :].unsqueeze(2).to_broadcast([1, MT, E]),
                                   tend[0:1, :].unsqueeze(1).to_broadcast([1, MT, E]), ALU.is_ge))
            settle()
            step(dve.scalar_tensor_tensor(adj[:, :], ntile[:, :], float(P), adj[:, :], ALU.mult, ALU.add))
            step(dve.tensor_reduce(tef[:, :], tge[:, :, :], AX.X, ALU.add))
            settle()
            step(dve.tensor_tensor(cum[:, :, :], cum[:, :, :], adj[:, :].unsqueeze(2).to_broadcast([P, E, NT]), ALU.add))
            step(dve.tensor_scalar(te[:, :], tef[:, :], float(E - 1), None, ALU.min))
            settle()
            step(dve.tensor_tensor(score[:, :, :], bank[6][:, 0:NT * E].rearrange("p (t e) -> p t e", e=E),
                                   cum[:, :, :].rearrange("p e t -> p t e"), ALU.add))
            settle()
            step(dve.tensor_tensor(score[:, :, :], score[:, :, :], hot[:, :, :], ALU.mult))
            settle()
            step(dve.tensor_reduce(slotf[:, :], score[:, :, :], AX.X, ALU.add))
            settle()
            dve.tensor_copy(slot[:, :], slotf[:, :]).then_inc(S["slots_ready"], 1)

            for j in range(NC):
                c, prev = slice(CH * j, CH * (j + 1)), slice(CH * j + 1, CH * (j + 1) + 1)
                dve.wait_ge(S["k_ready"], j + 1)
                settle()
                step(dve.tensor_tensor_scan(m_run[:, prev], decay[:, 0:1].to_broadcast([P, CH]), kf[:, c],
                                            m_run[:, CH * j:CH * j + 1], ALU.add, ALU.max))
                settle()
                step(dve.scalar_tensor_tensor(dd[:, c], kf[:, c], vec[:, 1:2], m_run[:, c], ALU.add, ALU.subtract))
                step(dve.scalar_tensor_tensor(arg[:, j, 0, :], m_run[:, c], decay[:, 0:1], m_run[:, prev], ALU.add, ALU.subtract))
                step(dve.tensor_tensor(arg[:, j, 1, :], kf[:, c], m_run[:, prev], ALU.subtract))
                settle()
                step(dve.tensor_scalar(arg[:, j, 2, :], dd[:, c], -1.0, 0.0, ALU.mult, ALU.min))
                dve.tensor_scalar(arg[:, j, 3, :], dd[:, c], 0.0, None, ALU.min).then_inc(S["wkv_args"], 1)
            for j in range(NC):
                c, prev = slice(CH * j, CH * (j + 1)), slice(CH * j + 1, CH * (j + 1) + 1)
                dve.wait_ge(S["wkv_exps"], j + 1)
                dve.wait_ge(S["v_ready"], j + 1)
                settle()
                step(dve.tensor_tensor(tmp, arg[:, j, 1, :], vf[:, c], ALU.mult))
                step(dve.tensor_tensor_scan(b_run[:, prev], arg[:, j, 0, :], arg[:, j, 1, :], b_run[:, CH * j:CH * j + 1], ALU.mult, ALU.add))
                settle()
                step(dve.tensor_tensor_scan(a_run[:, prev], arg[:, j, 0, :], tmp, a_run[:, CH * j:CH * j + 1], ALU.mult, ALU.add))
                settle()
                step(dve.tensor_tensor(tmp2, arg[:, j, 2, :], a_run[:, c], ALU.mult))
                step(dve.tensor_tensor(arg[:, j, 0, :], arg[:, j, 2, :], b_run[:, c], ALU.mult))
                step(dve.tensor_tensor(arg[:, j, 1, :], arg[:, j, 3, :], vf[:, c], ALU.mult))
                dve.wait_ge(S["e_ready"], j + 1)
                settle()
                step(dve.tensor_tensor(arg[:, j, 0, :], arg[:, j, 0, :], arg[:, j, 3, :], ALU.add))
                settle()
                step(dve.scalar_tensor_tensor(arg[:, j, 0, :], ef[:, c], 1.0, arg[:, j, 0, :], ALU.add, ALU.mult))
                step(dve.tensor_tensor(tmp2, tmp2, arg[:, j, 1, :], ALU.add))
                settle()
                step(dve.reciprocal(arg[:, j, 0, :], arg[:, j, 0, :]))
                settle()
                dve.tensor_tensor(buf_a[:, c], tmp2, arg[:, j, 0, :], ALU.mult).then_inc(S["rwkv_ready"], 1)
            dve.wait_ge(S["rwkv_ready"], NC)
            step(dve.memset(ks32, 0.0))
            settle()
            step(dve.memset(k_stack[0:2, 0, :], 1.0))
            step(dve.memset(k_stack[64:66, 1, :], 1.0))
            settle()
            dve.sem_inc(S["k_zeroed"], 1)
            for j in range(NC):
                xj = xs[:, TPC * j:TPC * (j + 1), :].rearrange("p n c -> p (n c)")
                dve.wait_ge(S["attn_mm"], j + 1)
                step(dve.tensor_tensor(xj, xj, bank[4 + j], ALU.add))
            dve.wait_ge(S["moe_y_mm"], MT)
            step(dve.memset(qs32[:, QZ:], 0.0))
            settle()
            dve.sem_inc(S["q_zeroed"], 1)
            dve.wait_ge(S["moe_in"], 16)
            for j in range(NC):
                xj = xs[:, TPC * j:TPC * (j + 1), :].rearrange("p n c -> p (n c)")
                settle()
                step(dve.tensor_tensor(xj, xj, buf_b[:, CH * j:CH * (j + 1)], ALU.add))
                settle()
                dve.sem_inc(S["x1_ready"], 1)
                tile_stats(j)
                if j:
                    normalise(j - 1, 1)
            normalise(NC - 1, 1)
            def norm_max(j):
                dve.wait_ge(S["norm_ready"], j + 1)
                step(dve.tensor_reduce(nmax[:, 0, j:j + 1], norm[:, CH * j:CH * (j + 1)], AX.X, ALU.max))
                dve.wait_ge(S["norm_mm"], 2 * j + 2)
                dve.tensor_reduce(nmax[:, 1, j:j + 1], bank[5][0:H, :], AX.X, ALU.max).then_inc(S["norms_read"], 1)

            for j in range(NC):
                for s in (1, 0):
                    p = piece[s][j]
                    dve.wait_ge(S["sq_ready"], 2 * j + 2 - s)
                    if j:
                        dve.wait_ge(S["piece_ready"], 2 * j - s)
                    step(dve.tensor_tensor(left[:, s, :], bank[2 + s], p[:, 0, :], ALU.subtract))
                    settle()
                    dve.tensor_copy(p[:, 1, :], left[:, s, :]).then_inc(S["middle_ready"], 1)
                if j:
                    norm_max(j - 1)
            norm_max(NC - 1)
            dve.wait_ge(S["norms_read"], NC)
            settle()
            step(dve.tensor_reduce(nbest[:, 0:2], nmax[:, :, :], AX.X, ALU.max))
            settle()
            dve.tensor_tensor(nbest[:, 2:3], nbest[:, 0:1], nbest[:, 1:2], ALU.add).then_inc(S["stack_set"], 1)
            def split_shift():
                settle()
                step(dve.tensor_copy(shiftp[:, 0, :], norm))
                settle()
                step(dve.tensor_tensor(shiftp[:, 1, :], norm, shiftp[:, 0, :], ALU.subtract))

            step(dve.tensor_scalar(norm, norm, nbest[:, 1:2], -0.5, ALU.add, ALU.mult))
            split_shift()
            dve.wait_ge(S["flag_mm"], 1)
            step(dve.tensor_reduce(flagf[:, :], bank[1][0:1, 0:H], AX.X, ALU.max))
            settle()
            dve.tensor_scalar(flag[:, :], flagf[:, :], SAFE, None, ALU.is_gt).then_inc(S["flag_ready"], 1)
            dve.wait_ge(S["flag_ready"], 1)
            wide = dve.value_load(flag[0:1, 0:1], min_val=0, max_val=1)
            with dve.If(wide):
                dve.sem_inc(S["gmax_read"], 1)
                with dve.Fori(0, H // 2) as g:
                    for half in range(2):
                        with dve.Fori(0, NT) as t:
                            dve.wait_ge(S["gmax_mm"], g * (2 * NT) + half * NT + t + 1)
                            dve.tensor_reduce(top[:, bass.ds(t, 1), bass.ds(g * 2 + half, 1)].rearrange("p a b -> p (a b)"),
                                              psum[:, 0:NC, :], AX.XY, ALU.max).then_inc(S["gmax_read"], 1)
                dve.wait_ge(S["gmax_turned"], 1)
                dve.tensor_scalar(norm, psum[0:H, 0:NC, :].rearrange("h a b -> h (a b)"), -1.0, None, ALU.mult).then_inc(S["gmax_read"], 1)
                dve.wait_ge(S["gmax_read"], H * NT + 2)
                dve.tensor_copy(shiftp[:, 0, :], norm).then_inc(S["wide_step"], 1)
                dve.wait_ge(S["wide_step"], 1)
                dve.tensor_tensor(shiftp[:, 1, :], norm, shiftp[:, 0, :], ALU.subtract).then_inc(S["wide_step"], 1)
                dve.wait_ge(S["wide_step"], 2)
            settle()
            dve.sem_inc(S["shift_ready"], 1)
            dve.sem_inc(S["acc_free"], 2)
            for j in range(NC):
                c = slice(CH * j, CH * (j + 1))
                dve.wait_ge(S["fe_ready"], j + 1)
                step(dve.tensor_scalar(buf_b[:, c], buf_b[:, c], 1.0, None, ALU.add))
                settle()
                step(dve.reciprocal(buf_b[:, c], buf_b[:, c]))
                dve.wait_ge(S["fkv_ready"], j + 1)
                settle()
                dve.tensor_tensor(buf_b[:, c], buf_b[:, c], buf_a[:, c], ALU.mult).then_inc(S["z_ready"], 1)
            base = n[0]
            for j in range(1, NC):
                dve.wait_ge(q_mid[j], 48)
            def divide(r, g):
                dve.wait_ge(S["pv_mm"], r * (G * NKT) + NKT * (g + 1))
                dve.wait_ge(y_packed[g % 2], r * (16 * HG * 2) + 16 * HG * (g // 2) + 16)
                dve.tensor_copy(y_g[:, g % 2, :], bank[6 + g % 2]).then_inc(S["acc_free"], 1)
                dve.wait_ge(S["acc_free"], r * G + g + 3)
                k = r * (3 * G) + (base + 3 * g)
                dve.wait_ge(S["dve_step"], k)
                dve.sem_inc(S["shuffle_turn"], 1)
                dve.stream_shuffle(y_den[:, :], y_g[:, g % 2, :], [HD] * 32).then_inc(S["dve_step"], 1)
                dve.wait_ge(S["dve_step"], k + 1)
                dve.reciprocal(y_den[:, :], y_den[:, :]).then_inc(S["dve_step"], 1)
                dve.wait_ge(S["dve_step"], k + 2)
                dve.tensor_tensor(y_g[:, g % 2, :], y_g[:, g % 2, :], y_den[:, :], ALU.mult).then_inc(S["dve_step"], 1)
                dve.wait_ge(S["dve_step"], k + 3)
                dve.sem_inc(S["y_ready"], 1)

            def finish(j, b):
                xj = xs[:, TPC * j:TPC * (j + 1), :].rearrange("p n c -> p (n c)")
                dve.wait_ge(S["proj_mm"], j + 1)
                dve.tensor_tensor(xj, xj, bank[b], ALU.add).then_inc(S["x1_ready"], 1)

            with dve.Fori(0, NQ - 1) as r:
                for g in range(G):
                    divide(r, g)
            divide(NQ - 1, 0)
            divide(NQ - 1, 1)
            finish(0, 7)
            finish(1, 7)
            dve.wait_ge(S["x1_ready"], NC + 2)
            dve.memset(bank[7], 0.0).then_inc(S["acc_zeroed"], 1)
            divide(NQ - 1, 2)
            finish(2, 6)
            dve.wait_ge(S["pv_mm"], NQ * G * NKT)
            dve.wait_ge(y_packed[1], 16 * HG * (2 * NQ - 1) + 16)
            dve.wait_ge(S["dve_step"], base + 3 * (G * NQ - 1))
            for half in range(2):
                c = slice(half * CH // 2, (half + 1) * CH // 2)
                k = 4 * half
                dve.tensor_copy(y_g[:, 1, c], bank[7][:, c]).then_inc(S["tail_step"], 1)
                dve.wait_ge(S["tail_step"], k + 1)
                dve.stream_shuffle(y_den[:, c], y_g[:, 1, c], [HD] * 32).then_inc(S["tail_step"], 1)
                dve.wait_ge(S["tail_step"], k + 2)
                dve.reciprocal(y_den[:, c], y_den[:, c]).then_inc(S["tail_step"], 1)
                dve.wait_ge(S["tail_step"], k + 3)
                dve.tensor_tensor(y_g[:, 1, c], y_g[:, 1, c], y_den[:, c], ALU.mult).then_inc(S["tail_step"], 1)
            for half in range(2):
                n = TPC * (NC - 1) + half * TPC // 2
                dve.wait_ge(S["proj_mm"], NC + half)
                dve.tensor_tensor(xs[:, n:n + TPC // 2, :], xs[:, n:n + TPC // 2, :],
                                  psum[:, half * TPC // 2:(half + 1) * TPC // 2, 0:C], ALU.add).then_inc(S["x1_ready"], 1)

        @block.tensor
        def _(pe):
            pe.wait_ge(S["ident_ready"], 1)

            def transposes(j, turn):
                pe.wait_ge(S["xn_ready"], turn * NC + j + 1)
                if j >= 2:
                    pe.wait_ge(S["xT_ready"], turn * NC + j - 1)
                for t in range(TPC):
                    mm = pe.transpose(bank[j % 2][:, P * t:P * (t + 1)], xn[:, TPC * j + t, 0:C], ident[:, :])
                mm.then_inc(S["xT_mm"], 1)

            def router(j):
                pe.wait_ge(S["xT_ready"], j + 1)
                for t in range(TPC * j, TPC * (j + 1)):
                    mm = pe.matmul(bank[5][:, E * t:E * (t + 1)], xnT[:, 1 + P * t:1 + P * (t + 1)], rw[:, :], start=True, stop=True)
                return mm

            transposes(0, 0)
            for j in range(NC):
                if j + 1 < NC:
                    transposes(j + 1, 0)
                if j == 0:
                    pe.wait_ge(S["const_in"], 32)
                    pe.wait_ge(S["dve_step"], 1)
                mm = router(j)
            mm.then_inc(S["router_mm"], 1)

            def mixed(b, w, j, done, freed):
                if j:
                    pe.wait_ge(freed, j)
                pe.matmul(bank[b], mix[:, w, 0, :], xnT[:, 1 + CH * j:1 + CH * (j + 1)], start=True, stop=False)
                pe.matmul(bank[b], mix[:, w, 1, :], xnT[:, CH * j:CH * (j + 1)], start=False, stop=True).then_inc(done, 1)

            pe.wait_ge(S["mix_ready"], 3)
            for j in range(NC):
                mixed(2, 0, j, S["k_mm"], S["k_ready"])
                if j == 0:
                    pe.wait_ge(S["hot_ready"], 1)
                    hot_f = hot[:, :, :].rearrange("p t e -> p (t e)")
                    pe.matmul(bank[6][:, 0:NT * E], before[:, :], hot_f, start=True, stop=True)
                    pe.matmul(bank[7][:, 0:NT * E], ones[:, :], hot_f, start=True, stop=True).then_inc(S["prefix_mm"], 1)
                mixed(3, 1, j, S["v_mm"], S["v_ready"])
                mixed(4, 2, j, S["r_mm"], S["e_ready"])

            def turn_x(i, s, fills, free=True):
                pe.wait_ge(rows_in[s], 16 * fills)
                if free:
                    pe.wait_ge(S["moe_xT_ready"], i)
                pe.transpose(bank[0][:, 0:P], xr[:, s, :], ident[:, :]).then_inc(S["moe_xT_mm"], 1)

            def up(i, s, fills):
                pe.wait_ge(w1_in[s], 16 * fills)
                pe.wait_ge(S["moe_xT_ready"], i + 1)
                for f in range(NF):
                    mm = pe.matmul(bank[5 + s][:, P * f:P * (f + 1)], w1[:, s, P * f:P * (f + 1)], xrT[:, s, :], start=True, stop=True)
                mm.then_inc(S["moe_h_mm"], 1)

            def down(i, s, free=True):
                e = pe.value_load(te[0:1, bass.ds(i, 1)], min_val=0, max_val=E - 1)
                if free:
                    pe.wait_ge(S["moe_y_ready"], i)
                pe.wait_ge(S["moe_h_ready"], i + 1)
                for f in range(NF):
                    pe.matmul(bank[1][:, 0:C], hT[:, s, P * f:P * (f + 1)], w2[:, bass.ds(e * F + C * f, C)], start=(f == 0), stop=False)
                pe.matmul(bank[1][:, 0:C], ones[0:1, :], b2[0:1, bass.ds(e * C, C)], start=False, stop=True).then_inc(S["moe_y_mm"], 1)

            pe.wait_ge(S["slots_ready"], 1)
            pe.wait_ge(S["experts_in"], 48)
            turn_x(0, 0, 1, False)
            turn_x(1, 1, 1)
            up(0, 0, 1)
            for i in range(RING):
                turn_x(i + 2, (i + 2) % RING, (i + 2) // RING + 1)
                up(i + 1, (i + 1) % RING, (i + 1) // RING + 1)
                down(i, i, i > 0)
            with pe.Fori(1, RUN) as r:
                for u in range(RING):
                    i = r * RING + u
                    turn_x(i + 2, (u + 2) % RING, r + (u + 2) // RING + 1)
                    up(i + 1, (u + 1) % RING, r + (u + 1) // RING + 1)
                    down(i, u)
            for i in range(RING * RUN, MT):
                if i + 2 < MT:
                    turn_x(i + 2, (i + 2) % RING, (i + 2) // RING + 1)
                if i + 1 < MT:
                    up(i + 1, (i + 1) % RING, (i + 1) // RING + 1)
                down(i, i % RING)
            for j in range(NC):
                pe.wait_ge(S["rwkv_ready"], j + 1)
                for t in range(TPC):
                    k = TPC * j + t
                    mm = pe.matmul(bank[4 + j][:, P * t:P * (t + 1)], buf_a[:, P * k:P * (k + 1)], wts[:, 3, :], start=True, stop=True)
                mm.then_inc(S["attn_mm"], 1)


            pe.wait_ge(S["wq_in"], 32)

            def norms(j):
                for s in range(2):
                    pe.wait_ge(S["sq_ready"], 2 * j + 2)
                    if s:
                        pe.wait_ge(S["norm_ready"], j + 1)
                    elif j:
                        pe.wait_ge(S["norms_read"], j)
                    pe.matmul(bank[5][0:H, :], headsel[:, :], sq[:, j % 2, s, :], start=True, stop=True).then_inc(S["norm_mm"], 1)

            def mixing(j, turn):
                w, done = ((4, "fk_mm"), (3, "fr_mm"))[turn]
                if turn == 0 and j >= 2:
                    pe.wait_ge(S["relu_ready"], j - 1)
                elif turn == 1:
                    pe.wait_ge(S["relu_ready"], NC)
                    if j >= 2:
                        pe.wait_ge(S["fe_ready"], j - 1)
                b = 6 + j % 2
                pe.matmul(bank[b], mix[:, w, 0, :], xnT[:, 1 + CH * j:1 + CH * (j + 1)], start=True, stop=False)
                pe.matmul(bank[b], mix[:, w, 1, :], xnT[:, CH * j:CH * (j + 1)], start=False, stop=True).then_inc(S[done], 1)

            def mixing_v(j):
                pe.wait_ge(S["kact_ready"], j + 1)
                if j >= 2:
                    pe.wait_ge(S["fkv_ready"], j - 1)
                pe.matmul(bank[2 + j % 2], wts[:, 6, :], buf_a[:, CH * j:CH * (j + 1)], start=True, stop=True).then_inc(S["fkv_mm"], 1)

            transposes(0, 1)
            for j in range(NC):
                if j + 1 < NC:
                    transposes(j + 1, 1)
                pe.wait_ge(S["xT_ready"], NC + j + 1)
                c = slice(1 + CH * j, 1 + CH * (j + 1))
                if j:
                    pe.wait_ge(S["middle_ready"], 2 * j)
                pe.matmul(bank[3], wqkv[:, C:2 * C], xnT[:, c], start=True, stop=True).then_inc(S["k2_mm"], 1)
                pe.matmul(bank[2], wqkv[:, 0:C], xnT[:, c], start=True, stop=True).then_inc(S["q_mm"], 1)
                if j:
                    pe.wait_ge(S["v_aug_ready"], j)
                for t in range(TPC):
                    k = TPC * j + t
                    mm = pe.matmul(bank[4][:, P * t:P * (t + 1)], xnT[:, 1 + P * k:1 + P * (k + 1)], wqkv[:, 2 * C:3 * C], start=True, stop=True)
                mm.then_inc(S["v2_mm"], 1)
                if j:
                    norms(j - 1)
                    mixing(j - 1, 0)
            norms(NC - 1)
            mixing(NC - 1, 0)
            mixing(0, 1)
            pe.wait_ge(S["stack_set"], 1)
            pe.transpose(bank[1][0:1, 0:H], nbest[:, 2:3], ident[0:H, 0:H]).then_inc(S["flag_mm"], 1)
            pe.wait_ge(S["middle_ready"], 2 * NC)
            for j in range(NC - 1):
                mixing_v(j)
                if j + 2 < NC:
                    mixing(j + 1, 1)
            pe.wait_ge(S["flag_ready"], 1)
            wide = pe.value_load(flag[0:1, 0:1], min_val=0, max_val=1)
            mixing_v(NC - 1)
            mixing(NC - 1, 1)
            pe.wait_ge(S["v_aug_ready"], NC)
            pe.wait_ge(S["norms_read"], NC)
            pe.wait_ge(S["fkv_ready"], NC)
            with pe.If(wide):
                pe.wait_ge(stack_in, 16 * (2 * NC + 2))
                pe.wait_ge(q_in, 32)
                pe.wait_ge(q_all_in, 32 * (NC - 1))
                with pe.Fori(0, H // 2) as g:
                    for half in range(2):
                        with pe.Fori(0, NT) as t:
                            pe.wait_ge(S["gmax_read"], g * (2 * NT) + half * NT + t + 1)
                            for b in range(NC):
                                mm = pe.matmul(bank[b], q_stack[:, bass.ds(g, 1), bass.ds(t * P, P)].rearrange("p a b -> p (a b)"),
                                               k_stack[:, bass.ds(g * 2 + half, 1), CH * b:CH * (b + 1)].rearrange("p a b -> p (a b)"),
                                               start=True, stop=True)
                            mm.then_inc(S["gmax_mm"], 1)
                pe.wait_ge(S["gmax_read"], H * NT + 1)
                for t in range(NT):
                    mm = pe.transpose(bank[t // TPC][0:H, P * (t % TPC):P * (t % TPC + 1)], top[:, t, :], ident[:, :])
                mm.then_inc(S["gmax_turned"], 1)
                pe.wait_ge(S["gmax_read"], H * NT + 2)
            pe.wait_ge(stack_in, 16 * (2 * NC + 2))
            pe.wait_ge(S["shift_in"], 32)

            def attend(r, u, project):
                g, kt = divmod(u, NKT)
                pe.wait_ge(S["exps_done"], r * (2 * G * NKT) + 2 * (u + 1))
                if project and u == 3 * NKT:
                    pe.wait_ge(S["acc_zeroed"], 1)
                if kt == 0:
                    pe.wait_ge(S["acc_free"], r * G + g + 1)
                for h in range(HG):
                    mm = pe.matmul(bank[6 + g % 2][32 * h:32 * h + HD + 1, :], v_aug[:, kt, HG * g + h, :], probs[:, u % 4, h, :],
                                   start=(kt == 0), stop=(kt == NKT - 1))
                mm.then_inc(S["pv_mm"], 1)

            def scores(r, u, wrap):
                g, kt = divmod(u, NKT)
                for half in range(2):
                    n = 2 * u + half
                    if n >= 3:
                        pe.wait_ge(S["exps_done"], r * (2 * G * NKT) + n - 2)
                    elif wrap and n < 2:
                        pe.wait_ge(S["exps_done"], r * (2 * G * NKT) + n - 1)
                    for h in range(2):
                        hh = HG * g + 2 * half + h
                        mm = pe.matmul(bank[2 * (n % 3) + h], k_stack[:, hh, P * kt:P * (kt + 1)],
                                       q_stack[:, hh // 2, bass.ds(r * CH, CH)], start=True, stop=True)
                    mm.then_inc(S["scores_mm"], 1)

            def project(j, b):
                for t in range(TPC):
                    k = TPC * j + t
                    pe.matmul(bank[b][:, P * t:P * (t + 1)], yT[:, P * k:P * (k + 1)], wo1[:, :], start=True, stop=False)
                    mm = pe.matmul(bank[b][:, P * t:P * (t + 1)], buf_b[:, P * k:P * (k + 1)], ident[:, :], start=False, stop=True)
                mm.then_inc(S["proj_mm"], 1)

            def query_block(r, last):
                for u in range(G * NKT):
                    if u + 1 < G * NKT:
                        scores(r, u + 1, False)
                    elif not last:
                        pe.wait_ge(q_in, r * 32 + 64)
                        scores(r + 1, 0, True)
                    attend(r, u, last)
                    if last and u == 2 * NKT + 1:
                        pe.wait_ge(S["acc_free"], r * G + 4)
                        pe.wait_ge(S["z_ready"], NC)
                        project(0, 7)
                    if last and u == 2 * NKT + 8:
                        pe.wait_ge(S["x1_ready"], NC + 1)
                        project(1, 7)
                    if last and u == 3 * NKT + 4:
                        pe.wait_ge(S["acc_free"], r * G + 5)
                        project(2, 6)

            pe.wait_ge(q_in, 32)
            scores(0, 0, False)
            pe.wait_ge(S["fe_ready"], NC)
            with pe.Fori(0, NQ - 1) as r:
                query_block(r, False)
            query_block(NQ - 1, True)
            pe.wait_ge(y_packed[0], 16 * HG * NQ * 2 + 16)
            pe.wait_ge(y_packed[1], 16 * HG * (2 * NQ - 1) + 16)
            pe.wait_ge(S["exps_done"], NQ * 2 * G * NKT)
            packed = HG * HD * (G - 1)
            for t in range(TPC):
                k = TPC * (NQ - 1) + t
                pe.matmul(bank[t][:, 0:C], buf_b[:, P * k:P * (k + 1)], ident[:, :], start=True, stop=False)
                pe.matmul(bank[t][:, 0:C], yT[0:packed, P * k:P * (k + 1)], wo1[0:packed, :], start=False, stop=False)
            pe.wait_ge(S["wo_last_in"], 16 * HG)
            for half in range(2):
                pe.wait_ge(S["tail_step"], 4 * half + 4)
                for t in range(half * TPC // 2, (half + 1) * TPC // 2):
                    mm = pe.matmul(bank[t][:, 0:C], y_g[:, 1, P * t:P * (t + 1)], wo_last[:, :], start=False, stop=True)
                mm.then_inc(S["proj_mm"], 1)


_OUTS = [((1, 2048, 128), "float32")]


def kernel(**inputs):
    import numpy as np
    import concourse.bacc as bacc
    from concourse import mybir as mb
    from concourse.bass_utils import run_bass_kernel_spmd as run

    a = {k: np.asarray(v) for k, v in inputs.items()}
    flat = lambda v: np.reshape(v, (-1,))
    vecs = np.stack([flat(a[k]) for k in ("L0_attn_W", "L0_attn_U", "L0_attn_time_mix_k", "L0_attn_time_mix_v",
                                          "L0_attn_time_mix_r", "L1_ffn_mu_r", "L1_ffn_mu_k")], axis=1)
    w_t = np.concatenate([a[k].T for k in ("L0_attn_Wk", "L0_attn_Wv", "L0_attn_Wr", "L0_attn_Wo",
                                           "L1_ffn_W_r", "L1_ffn_W_k", "L1_ffn_W_v")], axis=1)
    w1, b1, w2 = a["L0_ffn_w1"], a["L0_ffn_b1"], a["L0_ffn_w2"]
    e, f, h = w2.shape
    w2r = np.transpose(np.reshape(w2, (e, f // 128, 128, h)), (0, 2, 1, 3)).reshape(e, 128, f // 128 * h)
    b1r = np.transpose(np.reshape(b1, (e, f // 128, 128)), (0, 2, 1))
    expert_b1 = np.transpose(b1r, (1, 0, 2)).reshape(128, -1)
    arrays = {"in_x": a["L0_attn_x"], "in_vecs": vecs, "in_w_t": w_t, "in_router_w": a["L0_ffn_wr"],
              "in_router_b": a["L0_ffn_br"], "in_expert_w1": w1, "in_expert_w2": w2r, "in_expert_b1": expert_b1,
              "in_expert_b2": np.reshape(a["L0_ffn_b2"], (1, -1)),
              "in_w_qkv": a["L1_attn_w_qkv"], "in_w_out": a["L1_attn_w_out"]}
    arrays = {k: np.ascontiguousarray(v) for k, v in arrays.items()}
    nc = bacc.Bacc("TRN2", target_bir_lowering=False, num_devices=1)
    args = [nc.dram_tensor(k, v.shape, mb.dt.from_np(v.dtype), kind="ExternalInput").ap() for k, v in arrays.items()]
    for i, (shape, dtype) in enumerate(_OUTS):
        args.append(nc.dram_tensor(f"out_{i}", shape, mb.dt.from_np(np.dtype(dtype)), kind="ExternalOutput").ap())
    two_layer_kernel(nc, *args)
    r = run(nc, [arrays], core_ids=[0])
    return r.results[0]["out_0"]
```
